# Optimizing a Trainium2 kernel written in Bass

```python
import numpy as np
import jax
import jax.numpy as jnp

def _softmax(x, axis=-1):
    return jax.nn.softmax(x, axis=axis)

def _gelu(x):
    return jax.nn.gelu(x, approximate=True)

def _silu(x):
    return jax.nn.silu(x)

def _sigmoid(x):
    return jax.nn.sigmoid(x)

def _layernorm(x, axis=-1, eps=1e-05):
    m = jnp.mean(x, axis=axis, keepdims=True)
    v = jnp.var(x, axis=axis, keepdims=True)
    return (x - m) / jnp.sqrt(v + eps)

def _scatter_add(tgt, idx, src, axis=0):
    return tgt.at[idx].add(src)

def _segment_sum(src, seg, n):
    return jax.ops.segment_sum(src, seg, n)
kernel_name = 'mk_gnn_preln_d4_gnn_r32_d683fa'

def setup_inputs(seed: int=0):
    np.random.seed(seed)
    _w = jnp.asarray

    def _rec_inputs():
        import jax
        import jax.numpy as jnp
        _gk = jax.random.key(seed)
        x = -0.000202 + 1 * jax.random.normal(jax.random.fold_in(_gk, 1), (50000, 128), jnp.float32)
        src = jax.random.randint(jax.random.fold_in(_gk, 2), (25000,), 0, 50000, jnp.int32)
        dst = jax.random.randint(jax.random.fold_in(_gk, 3), (25000,), 0, 50000, jnp.int32)
        _o = jnp.argsort(dst, stable=True)
        src = src[_o]
        dst = dst[_o]
        edge_attr_9 = 0.000458729 + 1.00015 * jax.random.normal(jax.random.fold_in(_gk, 11), (25000, 9), jnp.float32)
        edge_type_16 = jax.random.randint(jax.random.fold_in(_gk, 13), (25000,), 0, 16, jnp.int32)
        edge_type_8 = jax.random.randint(jax.random.fold_in(_gk, 14), (25000,), 0, 8, jnp.int32)
        return (x, src, dst, edge_attr_9, edge_type_16, edge_type_8)
    x, src, dst, edge_attr_9, edge_type_16, edge_type_8 = _rec_inputs()

    def _L0_gnn_setup():
        import jax, jax.numpy as jnp
        import numpy as np
        N_NODES = 50000
        N_EDGES = 25000
        IN_DIM = 128
        OUT_DIM = 128
        N_REL = 8
        key = jax.random.key(seed)
        k1, k2, k3, k4, k5, k6 = jax.random.split(key, 6)
        x = jax.random.normal(k1, (N_NODES, IN_DIM), dtype=jnp.float32)
        edge_index = jax.random.randint(k2, (2, N_EDGES), 0, N_NODES, dtype=jnp.int64)
        edge_type = jax.random.randint(k3, (N_EDGES,), 0, N_REL, dtype=jnp.int64)
        scale = 1.0 / np.sqrt(IN_DIM)
        weight = jax.random.normal(k4, (N_REL, IN_DIM, OUT_DIM), dtype=jnp.float32) * scale
        root = jax.random.normal(k5, (IN_DIM, OUT_DIM), dtype=jnp.float32) * scale
        bias = jax.random.normal(k6, (OUT_DIM,), dtype=jnp.float32) * 0.01
        return {'x': x, 'edge_index': edge_index, 'edge_type': edge_type, 'weight': weight, 'root': root, 'bias': bias}
    _L0_gnn_all = _L0_gnn_setup()
    _L0_gnn_in = {k: v for k, v in _L0_gnn_all.items() if k in ('weight', 'root', 'bias')}
    del _L0_gnn_all

    def _L1_gnn_setup():
        import jax, jax.numpy as jnp
        import numpy as np
        N_NODES = 3125
        N_EDGES = 18750
        D_IN = 128
        D_OUT = 128
        N_REL = 16
        N_BASES = 2
        key = jax.random.key(seed)
        k1, k2, k3, k4, k5, k6 = jax.random.split(key, 6)
        x = jax.random.normal(k1, (N_NODES, D_IN), dtype=jnp.float32)
        edge_idx = jax.random.randint(k2, (2, N_EDGES), 0, N_NODES, dtype=jnp.int32)
        edge_type = jax.random.randint(k3, (N_EDGES,), 0, N_REL, dtype=jnp.int32)
        self_weight = jax.random.normal(k4, (D_IN, D_OUT), dtype=jnp.float32) * (2.0 / D_IN) ** 0.5
        bases = jax.random.normal(k5, (N_BASES, D_IN, D_OUT), dtype=jnp.float32) * (2.0 / (D_IN + D_OUT)) ** 0.5
        base_weights = jax.random.normal(k6, (N_REL, N_BASES), dtype=jnp.float32) * (2.0 / (N_REL + N_BASES)) ** 0.5
        return {'x': x, 'edge_idx': edge_idx, 'edge_type': edge_type, 'self_weight': self_weight, 'bases': bases, 'base_weights': base_weights}
    _L1_gnn_all = _L1_gnn_setup()
    _L1_gnn_in = {k: v for k, v in _L1_gnn_all.items() if k in ('self_weight', 'bases', 'base_weights')}
    del _L1_gnn_all

    def _L2_gnn_setup():
        import jax, jax.numpy as jnp
        import numpy as np
        from fractions import Fraction
        from math import factorial

        def _su2_cg_coeff(j1, m1, j2, m2, j3, m3):
            if m3 != m1 + m2:
                return 0.0
            vmin = int(max(-j1 + j2 + m3, -j1 + m1, 0))
            vmax = int(min(j2 + j3 + m1, j3 - j1 + j2, j3 + m3))
            f = lambda n: factorial(round(n))
            C = ((2.0 * j3 + 1.0) * Fraction(f(j3 + j1 - j2) * f(j3 - j1 + j2) * f(j1 + j2 - j3) * f(j3 + m3) * f(j3 - m3), f(j1 + j2 + j3 + 1) * f(j1 - m1) * f(j1 + m1) * f(j2 - m2) * f(j2 + m2))) ** 0.5
            S = 0
            for v in range(vmin, vmax + 1):
                S += (-1) ** (v + j2 + m2) * Fraction(f(j2 + j3 + m1 - v) * f(j1 - m1 + v), f(v) * f(j3 - j1 + j2 - v) * f(j3 + m3 - v) * f(v + j1 - j2 - m3))
            return float(C * S)

        def _change_basis_real_to_complex(l):
            q = np.zeros((2 * l + 1, 2 * l + 1), dtype=np.complex128)
            for m in range(-l, 0):
                q[l + m, l + abs(m)] = 1 / np.sqrt(2)
                q[l + m, l - abs(m)] = -1j / np.sqrt(2)
            q[l, l] = 1
            for m in range(1, l + 1):
                q[l + m, l + abs(m)] = (-1) ** m / np.sqrt(2)
                q[l + m, l - abs(m)] = 1j * (-1) ** m / np.sqrt(2)
            return (-1j) ** l * q

        def wigner_3j(l1, l2, l3):
            C = np.zeros((2 * l1 + 1, 2 * l2 + 1, 2 * l3 + 1))
            for m1 in range(-l1, l1 + 1):
                for m2 in range(-l2, l2 + 1):
                    m3 = m1 + m2
                    if abs(m3) <= l3:
                        C[l1 + m1, l2 + m2, l3 + m3] = _su2_cg_coeff(l1, m1, l2, m2, l3, m3)
            Q1 = _change_basis_real_to_complex(l1)
            Q2 = _change_basis_real_to_complex(l2)
            Q3 = _change_basis_real_to_complex(l3)
            Cc = np.einsum('ij,kl,mn,ikn->jlm', Q1, Q2, np.conj(Q3.T), C.astype(np.complex128))
            Cr = np.real(Cc)
            return Cr / np.linalg.norm(Cr)
        MUL = 32
        IRREPS_IN = [(MUL, 0, 1), (MUL, 1, -1)]
        IRREPS_SH = [(1, 0, 1), (1, 1, -1), (1, 2, 1)]
        IRREPS_OUT = [(MUL, 0, 1), (MUL, 1, -1)]
        NUM_NEIGHBORS = 10.0
        N_NODES, N_EDGES = (10000, 3125)

        def _dim(irreps):
            return sum((m * (2 * l + 1) for m, l, _ in irreps))

        def _slices(irreps):
            s, out = (0, [])
            for m, l, _ in irreps:
                d = m * (2 * l + 1)
                out.append((s, s + d))
                s += d
            return out

        def _instructions():
            ins = []
            for i1, (m1, l1, p1) in enumerate(IRREPS_IN):
                for i2, (m2, l2, p2) in enumerate(IRREPS_SH):
                    for io, (mo, lo, po) in enumerate(IRREPS_OUT):
                        if abs(l1 - l2) <= lo <= l1 + l2 and p1 * p2 == po:
                            ins.append((i1, i2, io))
            return ins
        _INSTR = _instructions()
        _SL_IN, _SL_SH, _SL_OUT = (_slices(IRREPS_IN), _slices(IRREPS_SH), _slices(IRREPS_OUT))
        _W3J = [jnp.asarray(wigner_3j(IRREPS_IN[i1][1], IRREPS_SH[i2][1], IRREPS_OUT[io][1]), dtype=jnp.float32) for i1, i2, io in _INSTR]
        _NORM = []
        for _i1, _i2, _io in _INSTR:
            _alpha = 2 * IRREPS_OUT[_io][1] + 1
            _x = sum((IRREPS_IN[j1][0] * IRREPS_SH[j2][0] for j1, j2, jo in _INSTR if jo == _io))
            _NORM.append(float(np.sqrt(_alpha / _x)))

        def _tensor_product(x1, x2, weights):
            E = x1.shape[0]
            out = jnp.zeros((E, _dim(IRREPS_OUT)), dtype=x1.dtype)
            for k, (i1, i2, io) in enumerate(_INSTR):
                m1, l1, _ = IRREPS_IN[i1]
                m2, l2, _ = IRREPS_SH[i2]
                mo, lo, _ = IRREPS_OUT[io]
                a, b = _SL_IN[i1]
                c, d = _SL_SH[i2]
                e, f = _SL_OUT[io]
                x1s = x1[:, a:b].reshape(E, m1, 2 * l1 + 1)
                x2s = x2[:, c:d].reshape(E, m2, 2 * l2 + 1)
                seg = jnp.einsum('uvw,ijk,eui,evj->ewk', weights[k], _W3J[k], x1s, x2s, optimize='optimal') * _NORM[k]
                out = out.at[:, e:f].add(seg.reshape(E, mo * (2 * lo + 1)))
            return out
        key = jax.random.key(seed)
        ks = jax.random.split(key, 8)
        x = jax.random.normal(ks[0], (N_NODES, _dim(IRREPS_IN)), dtype=jnp.float32)
        edge_index = jax.random.randint(ks[1], (2, N_EDGES), 0, N_NODES)
        edge_attr = jax.random.normal(ks[2], (N_EDGES, _dim(IRREPS_SH)), dtype=jnp.float32)
        ws = {f'w{k}': jax.random.normal(ks[3 + k], (MUL, 1, MUL), dtype=jnp.float32) for k in range(len(_INSTR))}
        return {'x': x, 'edge_index': edge_index, 'edge_attr': edge_attr, **ws}
    _L2_gnn_all = _L2_gnn_setup()
    _L2_gnn_in = {k: v for k, v in _L2_gnn_all.items() if k in ('w0', 'w1', 'w2', 'w3', 'w4')}
    del _L2_gnn_all

    def _L3_gnn_setup():
        import jax, jax.numpy as jnp
        import numpy as np
        N_NODES = 50000
        N_EDGES = 25000
        DIM = 128
        BN_EPS = 1e-05
        key = jax.random.key(seed)
        ks = jax.random.split(key, 12)
        d = DIM
        s = 1.0 / np.sqrt(d)
        x = jax.random.normal(ks[0], (N_NODES, d), dtype=jnp.float32)
        edge_index = jax.random.randint(ks[1], (2, N_EDGES), 0, N_NODES, dtype=jnp.int64)
        W_msg = jax.random.uniform(ks[2], (d, d), jnp.float32, -s, s)
        b_msg = jax.random.uniform(ks[3], (d,), jnp.float32, -s, s)
        sa = 1.0 / np.sqrt(2 * d)
        W_att = jax.random.uniform(ks[4], (2 * d, 1), jnp.float32, -sa, sa)
        b_att = jax.random.uniform(ks[5], (1,), jnp.float32, -sa, sa)
        W_ih = jax.random.uniform(ks[6], (3 * d, d), jnp.float32, -s, s)
        b_ih = jax.random.uniform(ks[7], (3 * d,), jnp.float32, -s, s)
        W_hh = jax.random.uniform(ks[8], (3 * d, d), jnp.float32, -s, s)
        b_hh = jax.random.uniform(ks[9], (3 * d,), jnp.float32, -s, s)
        gamma = jnp.ones((d,), jnp.float32)
        beta = jnp.zeros((d,), jnp.float32)
        return {'x': x, 'edge_index': edge_index, 'W_msg': W_msg, 'b_msg': b_msg, 'W_att': W_att, 'b_att': b_att, 'W_ih': W_ih, 'b_ih': b_ih, 'W_hh': W_hh, 'b_hh': b_hh, 'gamma': gamma, 'beta': beta}
    _L3_gnn_all = _L3_gnn_setup()
    _L3_gnn_in = {k: v for k, v in _L3_gnn_all.items() if k in ('W_msg', 'b_msg', 'W_att', 'b_att', 'W_ih', 'b_ih', 'W_hh', 'b_hh', 'gamma', 'beta')}
    del _L3_gnn_all
    return {'x': x, 'src': src, 'dst': dst, 'edge_attr_9': edge_attr_9, 'edge_type_16': edge_type_16, 'edge_type_8': edge_type_8, 'L0_gnn_weight': _L0_gnn_in['weight'], 'L0_gnn_root': _L0_gnn_in['root'], 'L0_gnn_bias': _L0_gnn_in['bias'], 'L1_gnn_self_weight': _L1_gnn_in['self_weight'], 'L1_gnn_bases': _L1_gnn_in['bases'], 'L1_gnn_base_weights': _L1_gnn_in['base_weights'], 'L2_gnn_w0': _L2_gnn_in['w0'], 'L2_gnn_w1': _L2_gnn_in['w1'], 'L2_gnn_w2': _L2_gnn_in['w2'], 'L2_gnn_w3': _L2_gnn_in['w3'], 'L2_gnn_w4': _L2_gnn_in['w4'], 'L3_gnn_W_msg': _L3_gnn_in['W_msg'], 'L3_gnn_b_msg': _L3_gnn_in['b_msg'], 'L3_gnn_W_att': _L3_gnn_in['W_att'], 'L3_gnn_b_att': _L3_gnn_in['b_att'], 'L3_gnn_W_ih': _L3_gnn_in['W_ih'], 'L3_gnn_b_ih': _L3_gnn_in['b_ih'], 'L3_gnn_W_hh': _L3_gnn_in['W_hh'], 'L3_gnn_b_hh': _L3_gnn_in['b_hh'], 'L3_gnn_gamma': _L3_gnn_in['gamma'], 'L3_gnn_beta': _L3_gnn_in['beta']}

def reference(x, src, dst, edge_attr_9, edge_type_16, edge_type_8, L0_gnn_weight, L0_gnn_root, L0_gnn_bias, L1_gnn_self_weight, L1_gnn_bases, L1_gnn_base_weights, L2_gnn_w0, L2_gnn_w1, L2_gnn_w2, L2_gnn_w3, L2_gnn_w4, L3_gnn_W_msg, L3_gnn_b_msg, L3_gnn_W_att, L3_gnn_b_att, L3_gnn_W_ih, L3_gnn_b_ih, L3_gnn_W_hh, L3_gnn_b_hh, L3_gnn_gamma, L3_gnn_beta):
    import jax
    import jax.numpy as jnp

    def _L0_gnn_ref(x, edge_index, edge_type, weight, root, bias):
        import jax, jax.numpy as jnp
        import numpy as np
        N_NODES = 50000
        N_EDGES = 25000
        IN_DIM = 128
        OUT_DIM = 128
        N_REL = 8
        src, dst = (edge_index[0], edge_index[1])
        h_src = x[src]
        out = x @ root + bias
        for r in range(N_REL):
            mask = (edge_type == r).astype(x.dtype)
            msg = h_src * mask[:, None] @ weight[r]
            agg = jax.ops.segment_sum(msg, dst, num_segments=N_NODES)
            cnt = jax.ops.segment_sum(mask, dst, num_segments=N_NODES)
            out = out + agg / jnp.maximum(cnt, 1.0)[:, None]
        return out

    def _L1_gnn_ref(x, edge_idx, edge_type, self_weight, bases, base_weights):
        import jax, jax.numpy as jnp
        import numpy as np
        N_NODES = 3125
        N_EDGES = 18750
        D_IN = 128
        D_OUT = 128
        N_REL = 16
        N_BASES = 2
        heads = edge_idx[0]
        tails = edge_idx[1]
        gathered = x[heads]
        n_rel = base_weights.shape[0]

        def work_relation(acc, rel_inputs):
            rel, coef = rel_inputs
            rel_mask = (edge_type == rel)[:, None]
            msgs = jnp.where(rel_mask, gathered, 0.0)
            scattered = jnp.zeros_like(x).at[tails].add(msgs)
            w_rel = jnp.einsum('b,bio->io', coef, bases)
            return (acc + scattered @ w_rel, None)
        init = jnp.zeros((x.shape[0], bases.shape[2]), dtype=x.dtype)
        rel_out, _ = jax.lax.scan(work_relation, init, (jnp.arange(n_rel, dtype=edge_type.dtype), base_weights))
        return x @ self_weight + rel_out

    def _L2_gnn_ref(x, edge_index, edge_attr, w0, w1, w2, w3, w4):
        import jax, jax.numpy as jnp
        import numpy as np
        from fractions import Fraction
        from math import factorial

        def _su2_cg_coeff(j1, m1, j2, m2, j3, m3):
            if m3 != m1 + m2:
                return 0.0
            vmin = int(max(-j1 + j2 + m3, -j1 + m1, 0))
            vmax = int(min(j2 + j3 + m1, j3 - j1 + j2, j3 + m3))
            f = lambda n: factorial(round(n))
            C = ((2.0 * j3 + 1.0) * Fraction(f(j3 + j1 - j2) * f(j3 - j1 + j2) * f(j1 + j2 - j3) * f(j3 + m3) * f(j3 - m3), f(j1 + j2 + j3 + 1) * f(j1 - m1) * f(j1 + m1) * f(j2 - m2) * f(j2 + m2))) ** 0.5
            S = 0
            for v in range(vmin, vmax + 1):
                S += (-1) ** (v + j2 + m2) * Fraction(f(j2 + j3 + m1 - v) * f(j1 - m1 + v), f(v) * f(j3 - j1 + j2 - v) * f(j3 + m3 - v) * f(v + j1 - j2 - m3))
            return float(C * S)

        def _change_basis_real_to_complex(l):
            q = np.zeros((2 * l + 1, 2 * l + 1), dtype=np.complex128)
            for m in range(-l, 0):
                q[l + m, l + abs(m)] = 1 / np.sqrt(2)
                q[l + m, l - abs(m)] = -1j / np.sqrt(2)
            q[l, l] = 1
            for m in range(1, l + 1):
                q[l + m, l + abs(m)] = (-1) ** m / np.sqrt(2)
                q[l + m, l - abs(m)] = 1j * (-1) ** m / np.sqrt(2)
            return (-1j) ** l * q

        def wigner_3j(l1, l2, l3):
            C = np.zeros((2 * l1 + 1, 2 * l2 + 1, 2 * l3 + 1))
            for m1 in range(-l1, l1 + 1):
                for m2 in range(-l2, l2 + 1):
                    m3 = m1 + m2
                    if abs(m3) <= l3:
                        C[l1 + m1, l2 + m2, l3 + m3] = _su2_cg_coeff(l1, m1, l2, m2, l3, m3)
            Q1 = _change_basis_real_to_complex(l1)
            Q2 = _change_basis_real_to_complex(l2)
            Q3 = _change_basis_real_to_complex(l3)
            Cc = np.einsum('ij,kl,mn,ikn->jlm', Q1, Q2, np.conj(Q3.T), C.astype(np.complex128))
            Cr = np.real(Cc)
            return Cr / np.linalg.norm(Cr)
        MUL = 32
        IRREPS_IN = [(MUL, 0, 1), (MUL, 1, -1)]
        IRREPS_SH = [(1, 0, 1), (1, 1, -1), (1, 2, 1)]
        IRREPS_OUT = [(MUL, 0, 1), (MUL, 1, -1)]
        NUM_NEIGHBORS = 10.0
        N_NODES, N_EDGES = (10000, 3125)

        def _dim(irreps):
            return sum((m * (2 * l + 1) for m, l, _ in irreps))

        def _slices(irreps):
            s, out = (0, [])
            for m, l, _ in irreps:
                d = m * (2 * l + 1)
                out.append((s, s + d))
                s += d
            return out

        def _instructions():
            ins = []
            for i1, (m1, l1, p1) in enumerate(IRREPS_IN):
                for i2, (m2, l2, p2) in enumerate(IRREPS_SH):
                    for io, (mo, lo, po) in enumerate(IRREPS_OUT):
                        if abs(l1 - l2) <= lo <= l1 + l2 and p1 * p2 == po:
                            ins.append((i1, i2, io))
            return ins
        _INSTR = _instructions()
        _SL_IN, _SL_SH, _SL_OUT = (_slices(IRREPS_IN), _slices(IRREPS_SH), _slices(IRREPS_OUT))
        _W3J = [jnp.asarray(wigner_3j(IRREPS_IN[i1][1], IRREPS_SH[i2][1], IRREPS_OUT[io][1]), dtype=jnp.float32) for i1, i2, io in _INSTR]
        _NORM = []
        for _i1, _i2, _io in _INSTR:
            _alpha = 2 * IRREPS_OUT[_io][1] + 1
            _x = sum((IRREPS_IN[j1][0] * IRREPS_SH[j2][0] for j1, j2, jo in _INSTR if jo == _io))
            _NORM.append(float(np.sqrt(_alpha / _x)))

        def _tensor_product(x1, x2, weights):
            E = x1.shape[0]
            out = jnp.zeros((E, _dim(IRREPS_OUT)), dtype=x1.dtype)
            for k, (i1, i2, io) in enumerate(_INSTR):
                m1, l1, _ = IRREPS_IN[i1]
                m2, l2, _ = IRREPS_SH[i2]
                mo, lo, _ = IRREPS_OUT[io]
                a, b = _SL_IN[i1]
                c, d = _SL_SH[i2]
                e, f = _SL_OUT[io]
                x1s = x1[:, a:b].reshape(E, m1, 2 * l1 + 1)
                x2s = x2[:, c:d].reshape(E, m2, 2 * l2 + 1)
                seg = jnp.einsum('uvw,ijk,eui,evj->ewk', weights[k], _W3J[k], x1s, x2s, optimize='optimal') * _NORM[k]
                out = out.at[:, e:f].add(seg.reshape(E, mo * (2 * lo + 1)))
            return out
        i, j = (edge_index[0], edge_index[1])
        summand = _tensor_product(x[i], edge_attr, [w0, w1, w2, w3, w4])
        out = jax.ops.segment_sum(summand, j, num_segments=x.shape[0])
        return out / float(np.sqrt(NUM_NEIGHBORS))

    def _L3_gnn_ref(x, edge_index, W_msg, b_msg, W_att, b_att, W_ih, b_ih, W_hh, b_hh, gamma, beta):
        import jax, jax.numpy as jnp
        import numpy as np
        N_NODES = 50000
        N_EDGES = 25000
        DIM = 128
        BN_EPS = 1e-05
        num_nodes, d = x.shape
        src = edge_index[0]
        dst = edge_index[1]
        xs = x[src]
        xd = x[dst]
        att = jax.nn.sigmoid(xs @ W_att[:d] + xd @ W_att[d:] + b_att)
        messages = (xs @ W_msg + b_msg) * att
        aggregated = jax.ops.segment_sum(messages, dst, num_segments=num_nodes)
        gi = aggregated @ W_ih.T + b_ih
        gh = x @ W_hh.T + b_hh
        i_r, i_z, i_n = jnp.split(gi, 3, axis=1)
        h_r, h_z, h_n = jnp.split(gh, 3, axis=1)
        r = jax.nn.sigmoid(i_r + h_r)
        z = jax.nn.sigmoid(i_z + h_z)
        n = jnp.tanh(i_n + r * h_n)
        h_new = (1.0 - z) * n + z * x
        mean = jnp.mean(h_new, axis=0)
        var = jnp.var(h_new, axis=0)
        return gamma * (h_new - mean) * jax.lax.rsqrt(var + BN_EPS) + beta
    edge_index = jnp.stack([src, dst])
    h = jnp.maximum(_layernorm(x, axis=-1), 0.0)
    x = x + _L0_gnn_ref(h, edge_index, edge_type_8, L0_gnn_weight, L0_gnn_root, L0_gnn_bias)
    h = jnp.maximum(_layernorm(x, axis=-1), 0.0)
    x = x + _L1_gnn_ref(h, edge_index, edge_type_16, L1_gnn_self_weight, L1_gnn_bases, L1_gnn_base_weights)
    h = jnp.maximum(_layernorm(x, axis=-1), 0.0)
    x = x + _L2_gnn_ref(h, edge_index, edge_attr_9, L2_gnn_w0, L2_gnn_w1, L2_gnn_w2, L2_gnn_w3, L2_gnn_w4)
    h = jnp.maximum(_layernorm(x, axis=-1), 0.0)
    x = x + _L3_gnn_ref(h, edge_index, L3_gnn_W_msg, L3_gnn_b_msg, L3_gnn_W_att, L3_gnn_b_att, L3_gnn_W_ih, L3_gnn_b_ih, L3_gnn_W_hh, L3_gnn_b_hh, L3_gnn_gamma, L3_gnn_beta)
    return x

_drawn_inputs = setup_inputs


def setup_inputs(seed=0):
    import zlib

    import numpy as np

    out = dict(_drawn_inputs(seed))
    spreads = {'L3_gnn_gamma': (1.0, 0.2), 'L3_gnn_beta': (0.0, 0.1)}
    factors = {'L0_gnn_bias': 7.521,
     'L3_gnn_b_msg': 5.96,
     'L3_gnn_W_att': 5.104,
     'L3_gnn_b_ih': 5.783,
     'L3_gnn_b_hh': 5.914}
    for name, (base, spread) in spreads.items():
        noise = np.random.default_rng([zlib.crc32(name.encode()), seed]).standard_normal(out[name].shape)
        drawn = base * np.exp(spread * noise) if base else spread * noise
        out[name] = jnp.asarray(drawn.astype(out[name].dtype))
    for name, factor in factors.items():
        out[name] = (out[name] * factor).astype(out[name].dtype)
    return out
```

```python
import math
from contextlib import ExitStack

import numpy as np

import concourse.bass as bass
from concourse import mybir
from concourse.alu_op_type import AluOpType as ALU

F32 = mybir.dt.float32
I32 = mybir.dt.int32
ACT = mybir.ActivationFunctionType
AX_X = mybir.AxisListType.X

P = 128
N_NODES, D = 50000, 128
N_EDGES = 25000
J = 4
GROUP = J * P
GROUPS = -(-N_NODES // GROUP)
ROWS = GROUPS * GROUP
ITERS = -(-N_EDGES // GROUP)
TILES = ITERS * J
EDGES = TILES * P
DUMP = ROWS - P
PAD_DST = DUMP - 1
TAIL = N_NODES - (GROUPS - 1) * GROUP
assert N_NODES <= PAD_DST
EPS = 1e-5
R0, R1, R2 = 8, 2, 9
N_TYPE16 = 16
PB = 512


def spherical_constants():
    def cg(j1, m1, j2, m2, j3, m3):
        if m3 != m1 + m2:
            return 0.0
        f = math.factorial
        vmin = max(-j1 + j2 + m3, -j1 + m1, 0)
        vmax = min(j2 + j3 + m1, j3 - j1 + j2, j3 + m3)
        c = math.sqrt((2 * j3 + 1) * f(j3 + j1 - j2) * f(j3 - j1 + j2) * f(j1 + j2 - j3)
                      * f(j3 + m3) * f(j3 - m3)
                      / (f(j1 + j2 + j3 + 1) * f(j1 - m1) * f(j1 + m1) * f(j2 - m2) * f(j2 + m2)))
        return c * sum((-1) ** (v + j2 + m2) * f(j2 + j3 + m1 - v) * f(j1 - m1 + v)
                       / (f(v) * f(j3 - j1 + j2 - v) * f(j3 + m3 - v) * f(v + j1 - j2 - m3))
                       for v in range(vmin, vmax + 1))

    def basis(l):
        q = np.zeros((2 * l + 1, 2 * l + 1), np.complex128)
        for m in range(-l, 0):
            q[l + m, l - m] = 1 / np.sqrt(2)
            q[l + m, l + m] = -1j / np.sqrt(2)
        q[l, l] = 1
        for m in range(1, l + 1):
            q[l + m, l + m] = (-1) ** m / np.sqrt(2)
            q[l + m, l - m] = 1j * (-1) ** m / np.sqrt(2)
        return (-1j) ** l * q

    def w3j(l1, l2, l3):
        c = np.zeros((2 * l1 + 1, 2 * l2 + 1, 2 * l3 + 1), np.complex128)
        for m1 in range(-l1, l1 + 1):
            for m2 in range(-l2, l2 + 1):
                if abs(m1 + m2) <= l3:
                    c[l1 + m1, l2 + m2, l3 + m1 + m2] = cg(l1, m1, l2, m2, l3, m1 + m2)
        r = np.real(np.einsum("ij,kl,mn,ikn->jlm", basis(l1), basis(l2), np.conj(basis(l3).T), c))
        return (r / np.linalg.norm(r)).astype(np.float32)

    n0 = math.sqrt(1.0 / 64) / math.sqrt(10.0)
    n1 = math.sqrt(3.0 / 96) / math.sqrt(10.0)
    out = np.zeros((P, R2, 4), np.float32)
    w000, w011, w101, w110, w121 = w3j(0, 0, 0), w3j(0, 1, 1), w3j(1, 0, 1), w3j(1, 1, 0), w3j(1, 2, 1)
    for p in range(P):
        if p < 32:
            out[p, 0, 0] = w000[0, 0, 0] * n0
            for j in range(3):
                out[p, 1 + j, 1:] = w011[0, j, :] * n1
        else:
            i = (p - 32) % 3
            out[p, 0, 1:] = w101[i, 0, :] * n1
            for j in range(3):
                out[p, 1 + j, 0] = w110[i, j, 0] * n0
            for j in range(5):
                out[p, 4 + j, 1:] = w121[i, j, :] * n1
    return out


def build(nc, x, src, dst, dst_flat, attr, type16, type8, w_rel, root, bias, self_w, bases, base_w,
          w0, w1, w2, w3, w4, w_msg, b_msg, w_att, b_att, w_ihT, b_ih, w_hhT, b_hh, gamma, beta,
          sph, out):
    with ExitStack() as ctx:
        def sb(name, *shape, dt=F32):
            return ctx.enter_context(nc.sbuf_tensor(name, list(shape), dt))

        phase_sems = []

        def sems(*names):
            new = [nc.alloc_semaphore(name=n) for n in names]
            phase_sems.extend(new)
            return new

        def end_phase():
            nc.clear_and_free_semaphores(phase_sems)
            phase_sems.clear()
            nc.all_engine_barrier()

        def table(name, rows, cols):
            return nc.dram_tensor(name, [rows, cols], F32, kind="Internal").ap()

        x1, x2, x3 = table("x1", ROWS, D), table("x2", ROWS, D), table("x3", ROWS, D)
        agg, counts = table("agg", ROWS, D), table("counts", ROWS, R0)
        newT = table("newT", D, ROWS)

        passed = ctx.enter_context(nc.semaphore("passed"))

        def wait_apart(eng, sem, value):
            eng.wait_ge(sem, value)
            eng.sem_inc(passed, 1)

        def first(it):
            return isinstance(it, int) and it == 0

        ident = sb("ident", P, P)
        before = sb("before", P, P)
        src_i, dst_i = sb("src_i", P, TILES, dt=I32), sb("dst_i", P, TILES, dt=I32)
        scat_i = sb("scat_i", P, TILES, dt=I32)
        src_now, dst_now = sb("src_now", P, 2, J, dt=I32), sb("dst_now", P, 2, J, dt=I32)
        scat_now = sb("scat_now", P, J, dt=I32)
        dst_f = sb("dst_f", P, TILES)
        dst_row = sb("dst_row", P, EDGES, dt=I32)
        dump_f = sb("dump_f", P, 1)
        repeat = sb("repeat", P, TILES)
        coef = sb("coef", P, TILES * R2)
        onehot = sb("onehot", P, TILES, R0)
        w_all = sb("w_all", P, R2 * P)
        b_row = sb("b_row", P, D)

        gx = sb("gx", P, 2, J, D)
        gd = sb("gd", P, 2, J, D)
        hs = sb("hs", P, 2, J, D)
        hd = sb("hd", P, J, D)
        hT = sb("hT", P, GROUP)
        aT = sb("aT", P, GROUP)
        prod = sb("prod", P, 2, R2 * D)
        msg = sb("msg", P, J, D)
        same = sb("same", P, J, P)
        comb = sb("comb", P, J, D)
        stats = sb("stats", P, 2 * J, 6)
        mv = sb("mv", P, 2 * J, 2)
        rstd, shift = sb("rstd", P, 2 * J), sb("shift", P, 2 * J)
        std = sb("std", P, 2 * J)
        att = sb("att", P, 3, J)
        psum = ctx.enter_context(nc.psum_tensor("psum", [P, 8, PB], F32))

        ld, const, step, rep = sems("set_ld", "set_const", "set_step", "set_rep")
        with nc.Block() as block:
            @block.sync
            def _(sp):
                sp.dma_start(src_i[:], src).then_inc(ld, 16)
                sp.dma_start(dst_i[:], dst).then_inc(ld, 16)
                sp.dma_start(dst_row[:], dst_flat.broadcast_to([P, EDGES])).then_inc(ld, 16)
                sp.dma_start(coef[:, 0:TILES].bitcast(I32), type8).then_inc(ld, 16)
                sp.dma_start(w_all[:, 0:R0 * P].rearrange("p (r o) -> p r o", r=R0),
                             w_rel.rearrange("r i o -> i r o")).then_inc(ld, 16)
                sp.dma_start(b_row[:], bias.broadcast_to([P, D])).then_inc(ld, 16)
                sp.wait_ge(ld, 96)

            @block.gpsimd
            def _(pool):
                pool.memset(ident[:], 0.0).then_inc(const, 1)
                pool.memset(before[:], 1.0).then_inc(const, 1)
                pool.iota(dump_f[:], [[0, 1]], base=DUMP, channel_multiplier=1,
                          allow_small_or_imprecise_dtypes=True).then_inc(const, 1)
                pool.wait_ge(const, 3)
                pool.affine_select(out=ident[:], in_=ident[:], compare_op=ALU.not_equal, fill=1.0,
                                   base=0, pattern=[[-1, P]], channel_multiplier=1).then_inc(const, 1)
                pool.affine_select(out=before[:], in_=before[:], compare_op=ALU.is_gt, fill=0.0,
                                   base=0, pattern=[[-1, P]], channel_multiplier=1).then_inc(const, 1)

            @block.vector
            def _(dve):
                dve.memset(onehot[:], 0.0).then_inc(step, 1)
                dve.wait_ge(ld, 96)
                dve.wait_ge(const, 5)
                dve.tensor_copy(dst_f[:], dst_i[:]).then_inc(step, 1)
                dve.wait_ge(step, 2)
                kind = coef[:, 0:TILES].bitcast(I32)
                for r in range(R0):
                    dve.tensor_scalar(onehot[:, :, r], kind, float(r), None, ALU.is_equal)
                with dve.Fori(0, ITERS) as it:
                    for k in range(J):
                        dve.scalar_tensor_tensor(
                            out=same[:, k, :], in0=dst_row[:, bass.ds(it * GROUP + k * P, P)],
                            scalar=dst_f[:, bass.ds(it * J + k, 1)], in1=before[:],
                            op0=ALU.is_equal, op1=ALU.mult).then_inc(rep, 1)
                    dve.wait_ge(rep, it * J + J)
                    dve.tensor_reduce(repeat[:, bass.ds(it * J, J)], same[:], AX_X,
                                      ALU.max).then_inc(step, 1)
                    dve.wait_ge(step, it + 3)
                dve.tensor_scalar(std[:, 0:1], dump_f[:], -1.0, None, ALU.mult).then_inc(step, 1)
                dve.wait_ge(step, ITERS + 3)
                dve.tensor_scalar(coef[:, 0:TILES], dst_f[:], std[:, 0:1], -1.0, ALU.add,
                                  ALU.mult).then_inc(step, 1)
                dve.wait_ge(step, ITERS + 4)
                dve.tensor_tensor(coef[:, 0:TILES], coef[:, 0:TILES], repeat[:], ALU.mult).then_inc(step, 1)
                dve.wait_ge(step, ITERS + 5)
                dve.tensor_tensor(scat_i[:], coef[:, 0:TILES], dst_f[:], ALU.add).then_inc(step, 1)
                dve.wait_ge(step, ITERS + 6)
        end_phase()

        zs, zd = sems("zero_set", "zero_dma")
        with nc.Block() as block:
            @block.vector
            def _(dve):
                dve.memset(gx[:], 0.0).then_inc(zs, 1)

            @block.sync
            def _(sp):
                sp.wait_ge(zs, 1)
                flat = gx[:].rearrange("p a j d -> p (a j d)")
                n = 0
                width = ROWS * R0 // P
                for at in range(0, width, 1024):
                    w = min(1024, width - at)
                    sp.dma_start(counts.rearrange("(p a) r -> p (a r)", p=P)[:, at:at + w],
                                 flat[:, 0:w]).then_inc(zd, 16)
                    n += 1
                with sp.Fori(0, GROUPS // 2) as it:
                    sp.dma_start(agg[bass.ds(it * 2 * GROUP, 2 * GROUP), :]
                                 .rearrange("(j p) d -> p j d", p=P),
                                 gx[:].rearrange("p a j d -> p (a j) d")).then_inc(zd, 16)
                sp.wait_ge(zd, 16 * (n + GROUPS // 2))
        end_phase()

        eq_s, pe_s, ev_s, sc_s, ix_s, free_s = sems("cnt_eq", "cnt_pe", "cnt_ev", "cnt_scat", "cnt_index",
                                                   "cnt_free")
        with nc.Block() as block:
            @block.vector
            def _(dve):
                with dve.Fori(0, ITERS) as it:
                    for k in range(J):
                        dve.tensor_scalar(same[:, k, :], dst_row[:, bass.ds(it * GROUP + k * P, P)],
                                          dst_f[:, bass.ds(it * J + k, 1)], None,
                                          ALU.is_equal).then_inc(eq_s, 1)
                    dve.wait_ge(pe_s, it * J + J)
                    dve.wait_ge(free_s, it + 1)
                    dve.tensor_copy(comb[:, :, 0:R0],
                                    psum[:, 0, 0:J * R0].rearrange("p (j r) -> p j r", j=J)).then_inc(ev_s, 1)

            @block.tensor
            def _(pe):
                with pe.Fori(0, ITERS) as it:
                    for k in range(J):
                        pe.wait_ge(eq_s, it * J + (k + 1))
                        pe.matmul(psum[:, 0, k * R0:(k + 1) * R0], same[:, k, :],
                                  onehot[:, bass.ds(it * J + k, 1), :].rearrange("p a r -> p (a r)"),
                                  start=True, stop=True).then_inc(pe_s, 1)

            @block.gpsimd
            def _(pool):
                pool.sem_inc(free_s, 1)
                with pool.Fori(0, ITERS) as it:
                    pool.tensor_copy(scat_now[:], scat_i[:, bass.ds(it * J, J)]).then_inc(ix_s, 1)
                    wait_apart(pool, ix_s, it + 1)
                    wait_apart(pool, ev_s, it + 1)
                    for k in range(J):
                        pool.indirect_dma_start(
                            counts, bass.IndirectOffsetOnAxis(scat_now[:, k:k + 1], 0),
                            comb[:, k, 0:R0], None, compute_op=ALU.add).then_inc(sc_s, 16)
                        wait_apart(pool, sc_s, it * (16 * J) + 16 * (k + 1))
                    pool.sem_inc(free_s, 1)
        end_phase()

        cg0, cg1, ci, cm, cc = sems("cof_ga0", "cof_ga1", "cof_index", "cof_mul", "cof_copy")
        with nc.Block() as block:
            cnt = coef[:, 0:TILES * R0]
            @block.gpsimd
            def _(pool):
                pool.sem_inc(cc, 2)

                def body(it, a):
                    pool.wait_ge(cc, it + 1)
                    pool.tensor_copy(dst_now[:, a, :], dst_i[:, bass.ds(it * J, J)]).then_inc(ci, 1)
                    wait_apart(pool, ci, it + 1)
                    for k in range(J):
                        pool.indirect_dma_start(gx[:, a, k, 0:R0], None, counts,
                                                bass.IndirectOffsetOnAxis(dst_now[:, a, k:k + 1], 0)
                                                ).then_inc((cg0, cg1)[a], 16)
                with pool.Fori(0, ITERS // 2) as pair:
                    for a in range(2):
                        body(pair * 2 + a, a)
                body(ITERS - 1, 0)

            @block.vector
            def _(dve):
                def body(it, pair, a):
                    dve.wait_ge((cg0, cg1)[a], pair * (16 * J) + 16 * J)
                    dve.tensor_copy(cnt[:, bass.ds(it * (J * R0), J * R0)].rearrange("p (j r) -> p j r", j=J),
                                    gx[:, a, :, 0:R0]).then_inc(cc, 1)
                with dve.Fori(0, ITERS // 2) as pair:
                    for a in range(2):
                        body(pair * 2 + a, pair, a)
                body(ITERS - 1, ITERS // 2, 0)
                dve.wait_ge(cc, ITERS + 2)
                oh = onehot[:].rearrange("p t r -> p (t r)")
                dve.tensor_scalar(cnt, cnt, 1.0, None, ALU.max).then_inc(cm, 1)
                dve.wait_ge(cm, 1)
                dve.reciprocal(cnt, cnt).then_inc(cm, 1)
                dve.wait_ge(cm, 2)
                dve.tensor_tensor(cnt, cnt, oh, ALU.mult).then_inc(cm, 1)
                dve.wait_ge(cm, 3)
        end_phase()

        def norm_dve(dve, s, rows, n, base, it, sq_waits):
            for k in range(n):
                dve.bn_stats(stats[:, k, :], rows(k)).then_inc(s["stat"], 1)
            wait_apart(dve, s["stat"], it * n + n)
            for k in range(n):
                ins = dve.bn_aggr(mv[:, k, :], stats[:, k, :])
                ins.then_inc(s["mv"], 1)
            dve.wait_ge(s["mv"], it * n + n)
            dve.tensor_scalar(std[:, 0:n], mv[:, 0:n, 1], EPS, None, ALU.add).then_inc(s["var"], 1)
            dve.wait_ge(s["std"], it + 1)
            dve.reciprocal(rstd[:, 0:n], std[:, 0:n]).then_inc(s["rstd"], 1)
            dve.wait_ge(s["rstd"], it + 1)
            dve.scalar_tensor_tensor(out=shift[:, 0:n], in0=mv[:, 0:n, 0], scalar=-1.0,
                                     in1=rstd[:, 0:n], op0=ALU.mult, op1=ALU.mult).then_inc(s["shift"], 1)

        def norm_act(act, s, n, it):
            act.wait_ge(s["var"], it + 1)
            act.activation(std[:, 0:n], std[:, 0:n], ACT.Sqrt).then_inc(s["std"], 1)
            act.wait_ge(s["shift"], it + 1)

        def norm_sems(name):
            names = ["stat", "mv", "var", "std", "rstd", "shift"]
            return dict(zip(names, sems(*[f"{name}_{n}" for n in names])))

        def dense_phase(name, x_in, x_out, w_dram, with_bias):
            s = norm_sems(name)
            w_ld, ld0, ld1, st0, st1, h_s, tr_s, ev_s, mm_s, res_s, xb_s = sems(
                *[f"{name}_{n}" for n in ("w", "ld0", "ld1", "st0", "st1", "h", "tr", "ev", "mm",
                                          "res", "xb")])
            loaded, stored = (ld0, ld1), (st0, st1)
            w = aT[:, 0:D]
            res = gd
            with nc.Block() as block:
                @block.sync
                def _(sp):
                    sp.dma_start(w, w_dram).then_inc(w_ld, 16)
                    sp.sem_inc(res_s, 2)
                    with sp.Fori(0, GROUPS // 2) as it:
                        for a in range(2):
                            sp.wait_ge(res_s, it * 2 + (a + 1))
                            sp.dma_start(gx[:, a], x_in[bass.ds((it * 2 + a) * GROUP, GROUP), :]
                                         .rearrange("(j p) d -> p j d", p=P)).then_inc(loaded[a], 16)

                @block.vector
                def _(dve):
                    def body(it):
                        for a in range(2):
                            g = it * 2 + a
                            dve.wait_ge(loaded[a], it * 16 + 16)
                            norm_dve(dve, s, lambda k: gx[:, a, k, :], J, 0, g, None)
                            dve.wait_ge(tr_s, g * J + J)
                            dve.tensor_copy(hT[:], psum[:, 0, :]).then_inc(ev_s, 1)
                            if with_bias:
                                for k in range(J):
                                    dve.tensor_tensor(prod[:, a, k * D:(k + 1) * D], gx[:, a, k, :],
                                                      b_row[:], ALU.add).then_inc(xb_s, 1)
                                dve.wait_ge(xb_s, g * J + J)
                                base = prod[:, a, 0:GROUP]
                            else:
                                base = gx[:, a].rearrange("p j d -> p (j d)")
                            dve.wait_ge(mm_s, g * J + J)
                            if not first(it):
                                dve.wait_ge(stored[a], it * 16)
                            dve.tensor_tensor(res[:, a].rearrange("p j d -> p (j d)"), psum[:, 1, :],
                                              base, ALU.add).then_inc(res_s, 1)
                    body(0)
                    with dve.Fori(1, GROUPS // 2) as it:
                        body(it)

                @block.scalar
                def _(act):
                    with act.Fori(0, GROUPS // 2) as it:
                        for a in range(2):
                            g = it * 2 + a
                            norm_act(act, s, J, g)
                            for k in range(J):
                                act.activation(hs[:, a, k, :], gx[:, a, k, :], ACT.Relu,
                                               bias=shift[:, k:k + 1], scale=rstd[:, k:k + 1]).then_inc(h_s, 1)
                            act.wait_ge(res_s, g + 3)
                            act.dma_start(x_out[bass.ds(g * GROUP, GROUP), :]
                                          .rearrange("(j p) d -> p j d", p=P), res[:, a]).then_inc(stored[a], 16)
                    for q in stored:
                        act.wait_ge(q, 16 * (GROUPS // 2))

                @block.tensor
                def _(pe):
                    pe.wait_ge(w_ld, 16)
                    with pe.Fori(0, GROUPS // 2) as it:
                        for a in range(2):
                            g = it * 2 + a
                            for k in range(J):
                                pe.wait_ge(h_s, g * J + (k + 1))
                                pe.transpose(psum[:, 0, k * P:(k + 1) * P], hs[:, a, k, :],
                                             ident[:]).then_inc(tr_s, 1)
                            pe.wait_ge(ev_s, g + 1)
                            for k in range(J):
                                pe.matmul(psum[:, 1, k * D:(k + 1) * D], hT[:, k * P:(k + 1) * P], w,
                                          start=True, stop=True).then_inc(mm_s, 1)
            end_phase()

        def edge_phase(name, x_in, x_out, products, gate=False):
            s = norm_sems(name)
            (ga0, ga1, h_s, tr_s, ev_s, mm_s, pr_s, msg_s, eq_s, sum_s, cb_s, sc_s, dot_s, gate_s,
             sig_s, ix_s, sx_s, free_s) = sems(
                *[f"{name}_{n}" for n in ("ga0", "ga1", "h", "tr", "ev", "mm", "prod", "msg", "eq",
                                          "sum", "comb", "scat", "dot", "gate", "sig", "index", "target", "free")])
            gathered = (ga0, ga1)
            n = 2 * J if gate else J
            per = (2 * J if gate else J)
            width = products * D
            banks = -(-width // PB)
            with nc.Block() as block:
                @block.gpsimd
                def _(pool):
                    def indices(it, a, count):
                        pool.tensor_copy(src_now[:, a, :], src_i[:, bass.ds(it * J, J)]).then_inc(ix_s, 1)
                        if gate:
                            pool.tensor_copy(dst_now[:, a, :], dst_i[:, bass.ds(it * J, J)]).then_inc(ix_s, 1)
                        wait_apart(pool, ix_s, count)

                    def gather(a, k):
                        pool.indirect_dma_start(gx[:, a, k, :], None, x_in,
                                                bass.IndirectOffsetOnAxis(src_now[:, a, k:k + 1], 0)
                                                ).then_inc(gathered[a], 16)
                        if gate:
                            pool.indirect_dma_start(gd[:, a, k, :], None, x_in,
                                                    bass.IndirectOffsetOnAxis(dst_now[:, a, k:k + 1], 0)
                                                    ).then_inc(gathered[a], 16)

                    lists = 2 if gate else 1

                    def body(it, a, more):
                        pool.tensor_copy(scat_now[:], scat_i[:, bass.ds(it * J, J)]).then_inc(sx_s, 1)
                        wait_apart(pool, sx_s, it + 1)
                        wait_apart(pool, cb_s, it + 1)
                        if more:
                            indices(it + 2, a, (it + 3) * lists)
                        for k in range(J):
                            pool.indirect_dma_start(x_out, bass.IndirectOffsetOnAxis(scat_now[:, k:k + 1], 0),
                                                    comb[:, k, :], None, compute_op=ALU.add).then_inc(sc_s, 16)
                            if more:
                                gather(a, k)
                            wait_apart(pool, sc_s, it * (16 * J) + 16 * (k + 1))
                        pool.sem_inc(free_s, 1)

                    pool.sem_inc(free_s, 1)
                    for a in range(2):
                        indices(a, a, (a + 1) * lists)
                        for k in range(J):
                            gather(a, k)
                    with pool.Fori(0, (ITERS - 3) // 2) as pair:
                        for a in range(2):
                            body(pair * 2 + a, a, True)
                    for it in range(ITERS - 3, ITERS):
                        body(it, it % 2, it + 2 < ITERS)

                def groups(engine, body):
                    with engine.Fori(0, ITERS // 2) as pair:
                        for a in range(2):
                            body(pair * 2 + a, pair, a)
                    body(ITERS - 1, ITERS // 2, 0)

                @block.vector
                def _(dve):
                    def body(it, pair, a):
                        dve.wait_ge(gathered[a], pair * (16 * per) + 16 * per)
                        norm_dve(dve, s, lambda k: gx[:, a, k, :] if k < J else gd[:, a, k - J, :],
                                 n, 0, it, None)
                        for k in range(J):
                            dve.tensor_scalar(same[:, k, :], dst_row[:, bass.ds(it * GROUP + k * P, P)],
                                              dst_f[:, bass.ds(it * J + k, 1)], None,
                                              ALU.is_equal).then_inc(eq_s, 1)
                        if gate:
                            dve.wait_ge(h_s, it * n + n)
                            for k in range(J):
                                for e, (h, w) in enumerate(((hs[:, a, k, :], w_all[:, 2 * D:3 * D]),
                                                            (hd[:, k, :], w_all[:, 3 * D:4 * D]))):
                                    dve.tensor_tensor_reduce(prod[:, e, k * D:(k + 1) * D], h, w, 1.0, 0.0,
                                                             ALU.mult, ALU.add, att[:, e, k:k + 1]).then_inc(dot_s, 1)
                            dve.wait_ge(dot_s, it * 2 * J + 2 * J)
                            dve.tensor_tensor(att[:, 2, :], att[:, 0, :], att[:, 1, :], ALU.add).then_inc(gate_s, 1)
                        dve.wait_ge(tr_s, it * J + J)
                        dve.tensor_copy(hT[:], psum[:, 0, :]).then_inc(ev_s, 1)
                        if gate:
                            dve.wait_ge(sig_s, it + 1)
                        for k in range(J):
                            t = it * J + k
                            dve.wait_ge(mm_s, t + 1)
                            b = 1 + 3 * (k % 2)
                            if gate:
                                dve.tensor_tensor(prod[:, k % 2, 0:D], psum[:, b, 0:D], w_all[:, D:2 * D],
                                                  ALU.add).then_inc(pr_s, 1)
                                dve.wait_ge(pr_s, t + 1)
                                dve.tensor_scalar(msg[:, k, :], prod[:, k % 2, 0:D], att[:, 2, k:k + 1],
                                                  None, ALU.mult).then_inc(msg_s, 1)
                                continue
                            ps = psum[:, b:b + 3, :].rearrange("p b c -> p (b c)")[:, 0:width]
                            cf = coef[:, bass.ds(t * products, products)]
                            dve.tensor_tensor(
                                prod[:, k % 2, 0:width].rearrange("p (r o) -> p r o", r=products),
                                ps.rearrange("p (r o) -> p r o", r=products),
                                cf.rearrange("p (r o) -> p r o", o=1).broadcast_to([P, products, D]),
                                ALU.mult).then_inc(pr_s, 1)
                            dve.wait_ge(pr_s, t + 1)
                            dve.tensor_reduce(msg[:, k, :],
                                              prod[:, k % 2, 0:width].rearrange("p (r o) -> p o r", r=products),
                                              AX_X, ALU.add).then_inc(msg_s, 1)
                        dve.wait_ge(sum_s, it * J + J)
                        dve.wait_ge(free_s, it + 1)
                        dve.tensor_copy(comb[:].rearrange("p j d -> p (j d)"), psum[:, 7, :]).then_inc(cb_s, 1)
                    groups(dve, body)

                @block.scalar
                def _(act):
                    def body(it, pair, a):
                        norm_act(act, s, n, it)
                        for k in range(n):
                            o = hs[:, a, k, :] if k < J else hd[:, k - J, :]
                            i = gx[:, a, k, :] if k < J else gd[:, a, k - J, :]
                            act.activation(o, i, ACT.Relu, bias=shift[:, k:k + 1],
                                           scale=rstd[:, k:k + 1]).then_inc(h_s, 1)
                        if gate:
                            act.wait_ge(gate_s, it + 1)
                            act.activation(att[:, 2, :], att[:, 2, :], ACT.Sigmoid,
                                           bias=w_all[:, 4 * D:4 * D + 1]).then_inc(sig_s, 1)
                    groups(act, body)

                @block.tensor
                def _(pe):
                    def body(it, pair, a):
                        for k in range(J):
                            pe.wait_ge(h_s, it * n + (k + 1))
                            pe.transpose(psum[:, 0, k * P:(k + 1) * P], hs[:, a, k, :],
                                         ident[:]).then_inc(tr_s, 1)
                        pe.wait_ge(ev_s, it + 1)

                        def combine(k):
                            pe.wait_ge(msg_s, it * J + (k + 1))
                            if k == 0:
                                pe.wait_ge(eq_s, it * J + J)
                            pe.matmul(psum[:, 7, k * D:(k + 1) * D], same[:, k, :], msg[:, k, :],
                                      start=True, stop=True).then_inc(sum_s, 1)

                        for k in range(J):
                            if k >= 2:
                                combine(k - 2)
                            b = 1 + 3 * (k % 2)
                            for q in range(banks):
                                lo, hi = q * PB, min((q + 1) * PB, width)
                                mm = pe.matmul(psum[:, b + q, 0:hi - lo], hT[:, k * P:(k + 1) * P],
                                               w_all[:, lo:hi], start=True, stop=True)
                            mm.then_inc(mm_s, 1)
                        combine(J - 2)
                        combine(J - 1)
                    groups(pe, body)
            end_phase()

        dense_phase("d0", x, x1, root, True)
        edge_phase("e0", x, x1, R0)

        ld1, c1 = sems("l1_ld", "l1_step")
        with nc.Block() as block:
            kind, acc = repeat[:].bitcast(I32), coef[:, 0:TILES * R1].rearrange("p (t b) -> p t b", b=R1)
            bw = prod[:, 0, 0:N_TYPE16 * R1]
            @block.sync
            def _(sp):
                sp.dma_start(kind, type16).then_inc(ld1, 16)
                sp.dma_start(bw, base_w.broadcast_to([P, N_TYPE16 * R1])).then_inc(ld1, 16)
                sp.dma_start(w_all[:, 0:R1 * D].rearrange("p (b o) -> p b o", b=R1),
                             bases.rearrange("b i o -> i b o")).then_inc(ld1, 16)
                sp.wait_ge(ld1, 48)

            @block.vector
            def _(dve):
                dve.wait_ge(ld1, 48)
                dve.memset(coef[:, 0:TILES * R1], 0.0).then_inc(c1, 1)
                dve.wait_ge(c1, 1)
                n = 1
                for r in range(N_TYPE16):
                    for b in range(R1):
                        w = bw[:, r * R1 + b:r * R1 + b + 1]
                        dve.tensor_scalar(onehot[:, :, b], kind, float(r), w, ALU.is_equal,
                                          ALU.mult).then_inc(c1, 1)
                    n += R1
                    dve.wait_ge(c1, n)
                    for b in range(R1):
                        dve.tensor_tensor(acc[:, :, b], acc[:, :, b], onehot[:, :, b], ALU.add).then_inc(c1, 1)
                    n += R1
                    dve.wait_ge(c1, n)
        end_phase()

        dense_phase("d1", x1, x2, self_w, False)
        edge_phase("e1", x1, x2, R1)

        ld2, c2, cp2 = sems("l2_ld", "l2_step", "l2_copy")
        with nc.Block() as block:
            spread = prod[:, 0, 0:5 * 32].rearrange("p (k w) -> p k w", k=5)
            sph_s = prod[:, 1, 0:R2 * 4].rearrange("p (m c) -> p m c", m=R2)
            wm = w_all[:].rearrange("p (m o) -> p m o", m=R2)

            @block.sync
            def _(sp):
                sp.dma_start(prod[:, 1, 0:R2 * 4], sph.rearrange("p m c -> p (m c)")).then_inc(ld2, 16)
                sp.dma_start(coef[:], attr).then_inc(ld2, 16)
                sp.wait_ge(c2, 1)
                for k, w in enumerate((w0, w1)):
                    sp.dma_start(spread[0:32, k, :], w.rearrange("u a w -> u (a w)")).then_inc(ld2, 16)
                for k, w in enumerate((w2, w3, w4)):
                    for i in range(3):
                        sp.dma_start(spread[32 + i:P:3, 2 + k, :],
                                     w.rearrange("u a w -> u (a w)")).then_inc(ld2, 16)
                with sp.Fori(0, GROUPS // 2) as it:
                    sp.dma_start(x3[bass.ds(it * 2 * GROUP, 2 * GROUP), :],
                                 x2[bass.ds(it * 2 * GROUP, 2 * GROUP), :]).then_inc(cp2, 16)
                sp.wait_ge(cp2, 16 * (GROUPS // 2))

            @block.vector
            def _(dve):
                dve.memset(prod[:, 0, 0:5 * 32], 0.0).then_inc(c2, 1)
                dve.wait_ge(ld2, 16 * 13)
                first = spread[:, 0, :]
                halves = spread[:, 1, :]
                for m in range(R2):
                    s0 = (0, 3)[m in (1, 2, 3)]
                    s1 = 2 if m == 0 else (1 if m < 4 else 4)
                    dve.tensor_scalar(wm[:, m, 0:32], spread[:, s0, :], sph_s[:, m, 0:1], None, ALU.mult)
                    for k in range(3):
                        dve.tensor_scalar(wm[:, m, 32 + k:D:3], spread[:, s1, :], sph_s[:, m, 1 + k:2 + k],
                                          None, ALU.mult)
                dve.drain()
        end_phase()

        edge_phase("e2", x2, x3, R2)

        (ld3,) = sems("l3_ld")
        with nc.Block() as block:
            @block.sync
            def _(sp):
                sp.dma_start(w_all[:, 0:D], w_msg).then_inc(ld3, 16)
                sp.dma_start(w_all[:, D:2 * D], b_msg.broadcast_to([P, D])).then_inc(ld3, 16)
                sp.dma_start(w_all[:, 2 * D:4 * D], w_att.broadcast_to([P, 2 * D])).then_inc(ld3, 16)
                sp.dma_start(w_all[:, 4 * D:4 * D + 1], b_att.broadcast_to([P, 1])).then_inc(ld3, 16)
                sp.wait_ge(ld3, 64)
        end_phase()
        edge_phase("e3", x3, agg, 1, gate=True)

        s = norm_sems("u")
        (w_ld, b_st, ld0, ld1_, st0, st1, h_s, tr_s, ev_s, mm_s, r_s, z_s, t1_s, t2_s, n_s, d_s, e_s, new_s,
         bn_s) = sems(*[f"u_{n}" for n in ("w", "b", "ld0", "ld1", "st0", "st1", "h", "tr", "ev", "mm", "r", "z",
                                           "t1", "t2", "n", "d", "e", "new", "bn")])
        loaded, stored = (ld0, ld1_), (st0, st1)
        wi, wh = w_all[:, 0:3 * D], w_all[:, 3 * D:6 * D]
        bvec = att[:].rearrange("p a b -> p (a b)")
        rg, zg, ng, tg = (prod[:, 0, 0:GROUP], prod[:, 0, GROUP:2 * GROUP],
                          prod[:, 1, 0:GROUP], prod[:, 1, GROUP:2 * GROUP])
        bn_st = coef[:, 0:GROUPS * 6].rearrange("p (g c) -> p g c", c=6)
        new = [msg[:].rearrange("p j d -> p (j d)"), same[:].rearrange("p j d -> p (j d)")]
        with nc.Block() as block:
            @block.sync
            def _(sp):
                sp.dma_start(wi, w_ihT).then_inc(w_ld, 16)
                sp.dma_start(wh, w_hhT).then_inc(w_ld, 16)
                sp.dma_start(bvec[:, 0:3], b_ih).then_inc(w_ld, 16)
                sp.dma_start(bvec[:, 3:6], b_hh).then_inc(w_ld, 16)
                sp.sem_inc(tr_s, 2)
                with sp.Fori(0, GROUPS // 2) as it:
                    for a in range(2):
                        g = it * 2 + a
                        sp.wait_ge(tr_s, g + 1)
                        for buf, tab in ((gx, x3), (gd, agg)):
                            sp.dma_start(buf[:, a], tab[bass.ds(g * GROUP, GROUP), :]
                                         .rearrange("(j p) d -> p j d", p=P)).then_inc(loaded[a], 16)

            @block.scalar
            def _(act):
                act.wait_ge(b_st, 1)
                with act.Fori(0, GROUPS // 2) as it:
                    for a in range(2):
                        g = it * 2 + a
                        norm_act(act, s, J, g)
                        for k in range(J):
                            act.activation(hs[:, a, k, :], gx[:, a, k, :], ACT.Relu,
                                           bias=shift[:, k:k + 1], scale=rstd[:, k:k + 1]).then_inc(h_s, 1)
                        act.wait_ge(mm_s, g + 1)
                        act.activation(rg, psum[:, 2, :], ACT.Sigmoid, bias=bvec[:, 6:7]).then_inc(r_s, 1)
                        act.activation(zg, psum[:, 3, :], ACT.Sigmoid, bias=bvec[:, 7:8]).then_inc(z_s, 1)
                        act.wait_ge(t2_s, g + 1)
                        act.activation(ng, tg, ACT.Tanh, bias=bvec[:, 2:3]).then_inc(n_s, 1)
                        act.wait_ge(new_s, g + 1)
                        act.dma_start(newT[:, bass.ds(g * GROUP, GROUP)], new[a]).then_inc(stored[a], 16)
                for q in stored:
                    act.wait_ge(q, 16 * (GROUPS // 2))

            @block.vector
            def _(dve):
                dve.wait_ge(w_ld, 64)
                dve.tensor_tensor(bvec[:, 6:8], bvec[:, 0:2], bvec[:, 3:5], ALU.add).then_inc(b_st, 1)
                def body(it):
                    for a in range(2):
                        g = it * 2 + a
                        dve.wait_ge(loaded[a], it * 32 + 32)
                        norm_dve(dve, s, lambda k: gx[:, a, k, :], J, 0, g, None)
                        dve.wait_ge(tr_s, g + 3)
                        dve.tensor_copy(hT[:], psum[:, 0, :]).then_inc(ev_s, 1)
                        dve.tensor_copy(aT[:], psum[:, 1, :]).then_inc(ev_s, 1)
                        dve.wait_ge(r_s, g + 1)
                        dve.scalar_tensor_tensor(out=tg, in0=psum[:, 5, :], scalar=bvec[:, 5:6], in1=rg,
                                                 op0=ALU.add, op1=ALU.mult).then_inc(t1_s, 1)
                        dve.wait_ge(t1_s, g + 1)
                        dve.tensor_tensor(tg, psum[:, 4, :], tg, ALU.add).then_inc(t2_s, 1)
                        dve.wait_ge(n_s, g + 1)
                        if not first(it):
                            dve.wait_ge(stored[a], it * 16)
                        dve.tensor_tensor(tg, hT[:], ng, ALU.subtract).then_inc(d_s, 1)
                        dve.wait_ge(d_s, g + 1)
                        dve.tensor_tensor(tg, tg, zg, ALU.mult).then_inc(e_s, 1)
                        dve.wait_ge(e_s, g + 1)
                        dve.tensor_tensor(new[a], tg, ng, ALU.add).then_inc(new_s, 1)
                        dve.wait_ge(new_s, g + 1)
                        dve.bn_stats(bn_st[:, bass.ds(g, 1), :].rearrange("p a c -> p (a c)"),
                                     new[a]).then_inc(bn_s, 1)
                body(0)
                with dve.Fori(1, GROUPS // 2) as it:
                    body(it)

                dve.wait_ge(bn_s, GROUPS)
                dve.bn_stats(bn_st[:, GROUPS - 1, :], new[(GROUPS - 1) % 2][:, 0:TAIL]).then_inc(bn_s, 1)
                dve.wait_ge(bn_s, GROUPS + 1)

            @block.tensor
            def _(pe):
                pe.wait_ge(w_ld, 64)
                with pe.Fori(0, GROUPS // 2) as it:
                    for a in range(2):
                        g = it * 2 + a
                        for k in range(J):
                            if k == 0:
                                pe.wait_ge(loaded[a], it * 32 + 32)
                            pe.transpose(psum[:, 1, k * P:(k + 1) * P], gd[:, a, k, :], ident[:])
                        for k in range(J):
                            pe.wait_ge(h_s, g * J + (k + 1))
                            mm = pe.transpose(psum[:, 0, k * P:(k + 1) * P], hs[:, a, k, :], ident[:])
                        mm.then_inc(tr_s, 1)
                        pe.wait_ge(ev_s, g * 2 + 2)
                        for q, (bank, src_m) in enumerate(((2, "ih"), (3, "ih"), (4, "i"), (5, "h"))):
                            col = min(q, 2) * D
                            if "i" in src_m:
                                mm = pe.matmul(psum[:, bank, :], wi[:, col:col + D], aT[:], start=True,
                                               stop=src_m == "i")
                            if "h" in src_m:
                                mm = pe.matmul(psum[:, bank, :], wh[:, col:col + D], hT[:],
                                               start=src_m == "h", stop=True)
                        mm.then_inc(mm_s, 1)
        end_phase()

        (f_ld, v_s, sd_s, ld0, ld1_, st0, st1, y_s, tr_s, res_s) = sems(
            *[f"f_{n}" for n in ("ld", "v", "sd", "ld0", "ld1", "st0", "st1", "y", "tr", "res")])
        loaded, stored = (ld0, ld1_), (st0, st1)
        gb = att[:].rearrange("p a b -> p (a b)")
        with nc.Block() as block:
            @block.sync
            def _(sp):
                sp.dma_start(gb[:, 0:1], gamma).then_inc(f_ld, 16)
                sp.dma_start(gb[:, 1:2], beta).then_inc(f_ld, 16)
                sp.sem_inc(res_s, 2)
                with sp.Fori(0, GROUPS // 2) as it:
                    for a in range(2):
                        g = it * 2 + a
                        sp.wait_ge(res_s, g + 1)
                        sp.dma_start(gx[:, a], x3[bass.ds(g * GROUP, GROUP), :]
                                     .rearrange("(j p) d -> p j d", p=P)).then_inc(loaded[a], 16)
                        sp.dma_start(gd[:, a].rearrange("p j d -> p (j d)"),
                                     newT[:, bass.ds(g * GROUP, GROUP)]).then_inc(loaded[a], 16)

            @block.scalar
            def _(act):
                act.wait_ge(v_s, 2)
                act.activation(std[:, 0:1], std[:, 0:1], ACT.Sqrt).then_inc(sd_s, 1)
                act.wait_ge(v_s, 5)
                with act.Fori(0, GROUPS // 2) as it:
                    for a in range(2):
                        g = it * 2 + a
                        act.wait_ge(loaded[a], it * 32 + 32)
                        act.activation(hs[:, a].rearrange("p j d -> p (j d)"),
                                       gd[:, a].rearrange("p j d -> p (j d)"), ACT.Identity,
                                       bias=gb[:, 3:4], scale=gb[:, 2:3]).then_inc(y_s, 1)
                        act.wait_ge(res_s, g + 3)
                        act.dma_start(out[bass.ds(g * GROUP, GROUP), :].rearrange("(j p) d -> p j d", p=P),
                                      comb[:] if a else msg[:]).then_inc(stored[a], 16)
                for q in stored:
                    act.wait_ge(q, 16 * (GROUPS // 2))

            @block.tensor
            def _(pe):
                with pe.Fori(0, GROUPS // 2) as it:
                    for a in range(2):
                        g = it * 2 + a
                        pe.wait_ge(y_s, g + 1)
                        pe.wait_ge(res_s, g + 1)
                        for k in range(J):
                            mm = pe.transpose(psum[:, a, k * P:(k + 1) * P], hs[:, a, k, :], ident[:])
                        mm.then_inc(tr_s, 1)

            @block.vector
            def _(dve):
                dve.wait_ge(f_ld, 32)
                dve.bn_aggr(mv[:, 0, :], coef[:, 0:GROUPS * 6]).then_inc(v_s, 1)
                dve.wait_ge(v_s, 1)
                dve.tensor_scalar(std[:, 0:1], mv[:, 0, 1:2], EPS, None, ALU.add).then_inc(v_s, 1)
                dve.wait_ge(sd_s, 1)
                dve.reciprocal(rstd[:, 0:1], std[:, 0:1]).then_inc(v_s, 1)
                dve.wait_ge(v_s, 3)
                dve.tensor_tensor(gb[:, 2:3], rstd[:, 0:1], gb[:, 0:1], ALU.mult).then_inc(v_s, 1)
                dve.wait_ge(v_s, 4)
                dve.scalar_tensor_tensor(out=shift[:, 0:1], in0=mv[:, 0, 0:1], scalar=-1.0,
                                         in1=gb[:, 2:3], op0=ALU.mult, op1=ALU.mult).then_inc(f_ld, 1)
                dve.wait_ge(f_ld, 33)
                dve.tensor_tensor(gb[:, 3:4], gb[:, 1:2], shift[:, 0:1], ALU.add).then_inc(v_s, 1)
                def body(it):
                    for a in range(2):
                        g = it * 2 + a
                        dve.wait_ge(tr_s, g + 1)
                        if not first(it):
                            dve.wait_ge(stored[a], it * 16)
                        dve.tensor_tensor((comb if a else msg)[:].rearrange("p j d -> p (j d)"), psum[:, a, :],
                                          gx[:, a].rearrange("p j d -> p (j d)"), ALU.add).then_inc(res_s, 1)
                body(0)
                with dve.Fori(1, GROUPS // 2) as it:
                    body(it)

        end_phase()


def kernel(**inputs):
    import numpy as _np
    import concourse.bacc as _bacc
    from concourse import mybir as _mybir
    from concourse.bass_utils import run_bass_kernel_spmd as _run

    def by_tile(a, fill):
        a = _np.asarray(a)
        pad = _np.full((EDGES - N_EDGES,) + a.shape[1:], fill, a.dtype)
        a = _np.concatenate([a, pad]).reshape((TILES, P) + a.shape[1:])
        return _np.ascontiguousarray(_np.moveaxis(a, 0, 1)).reshape(P, -1)

    i = {k: _np.asarray(v) for k, v in inputs.items()}
    cols = lambda a, n: _np.ascontiguousarray(a.reshape(n, -1).T)
    arrays = {
        "x": _np.concatenate([i["x"], _np.zeros((ROWS - N_NODES, D), i["x"].dtype)]),
        "src": by_tile(i["src"], 0), "dst": by_tile(i["dst"], PAD_DST),
        "dst_flat": _np.concatenate([i["dst"], _np.full(EDGES - N_EDGES, PAD_DST, i["dst"].dtype)])[None],
        "attr": by_tile(i["edge_attr_9"], 0), "type16": by_tile(i["edge_type_16"], 0),
        "type8": by_tile(i["edge_type_8"], 0).view(_np.int32),
        "w_rel": i["L0_gnn_weight"], "root": i["L0_gnn_root"], "bias": i["L0_gnn_bias"][None],
        "self_w": i["L1_gnn_self_weight"], "bases": i["L1_gnn_bases"],
        "base_w": i["L1_gnn_base_weights"].reshape(1, -1),
        **{f"w{k}": i[f"L2_gnn_w{k}"] for k in range(5)},
        "w_msg": i["L3_gnn_W_msg"], "b_msg": i["L3_gnn_b_msg"][None], "w_att": i["L3_gnn_W_att"].reshape(1, -1),
        "b_att": i["L3_gnn_b_att"][None], "w_ihT": _np.ascontiguousarray(i["L3_gnn_W_ih"].T),
        "b_ih": cols(i["L3_gnn_b_ih"], 3), "w_hhT": _np.ascontiguousarray(i["L3_gnn_W_hh"].T),
        "b_hh": cols(i["L3_gnn_b_hh"], 3), "gamma": i["L3_gnn_gamma"][:, None], "beta": i["L3_gnn_beta"][:, None],
        "sph": spherical_constants(),
    }
    nc = _bacc.Bacc("TRN2", target_bir_lowering=False, num_devices=1)
    feed, args = {}, {}
    for name, a in arrays.items():
        a = _np.ascontiguousarray(a)
        dt = I32 if a.dtype == _np.int32 else F32
        feed[f"in_{name}"] = a
        args[name] = nc.dram_tensor(f"in_{name}", a.shape, dt, kind="ExternalInput").ap()
    out = nc.dram_tensor("out_x", (ROWS, D), F32, kind="ExternalOutput").ap()
    build(nc, out=out, **args)
    r = _run(nc, [feed], core_ids=[0])
    return r.results[0]["out_x"][:N_NODES]
```

```python
import math
from contextlib import ExitStack

import numpy as np

import concourse.bass as bass
from concourse import mybir
from concourse.alu_op_type import AluOpType as ALU

F32 = mybir.dt.float32
I32 = mybir.dt.int32
ACT = mybir.ActivationFunctionType
AX_X = mybir.AxisListType.X

P = 128
N_NODES, D = 50000, 128
N_EDGES = 25000
J = 4
GROUP = J * P
GROUPS = -(-N_NODES // GROUP)
ROWS = GROUPS * GROUP
ITERS = -(-N_EDGES // GROUP)
TILES = ITERS * J
EDGES = TILES * P
DUMP = ROWS - P
PAD_DST = DUMP - 1
TAIL = N_NODES - (GROUPS - 1) * GROUP
assert N_NODES <= PAD_DST
EPS = 1e-5
R0, R1, R2 = 8, 2, 9
N_TYPE16 = 16
PB = 512


def spherical_constants():
    def cg(j1, m1, j2, m2, j3, m3):
        if m3 != m1 + m2:
            return 0.0
        f = math.factorial
        vmin = max(-j1 + j2 + m3, -j1 + m1, 0)
        vmax = min(j2 + j3 + m1, j3 - j1 + j2, j3 + m3)
        c = math.sqrt((2 * j3 + 1) * f(j3 + j1 - j2) * f(j3 - j1 + j2) * f(j1 + j2 - j3)
                      * f(j3 + m3) * f(j3 - m3)
                      / (f(j1 + j2 + j3 + 1) * f(j1 - m1) * f(j1 + m1) * f(j2 - m2) * f(j2 + m2)))
        return c * sum((-1) ** (v + j2 + m2) * f(j2 + j3 + m1 - v) * f(j1 - m1 + v)
                       / (f(v) * f(j3 - j1 + j2 - v) * f(j3 + m3 - v) * f(v + j1 - j2 - m3))
                       for v in range(vmin, vmax + 1))

    def basis(l):
        q = np.zeros((2 * l + 1, 2 * l + 1), np.complex128)
        for m in range(-l, 0):
            q[l + m, l - m] = 1 / np.sqrt(2)
            q[l + m, l + m] = -1j / np.sqrt(2)
        q[l, l] = 1
        for m in range(1, l + 1):
            q[l + m, l + m] = (-1) ** m / np.sqrt(2)
            q[l + m, l - m] = 1j * (-1) ** m / np.sqrt(2)
        return (-1j) ** l * q

    def w3j(l1, l2, l3):
        c = np.zeros((2 * l1 + 1, 2 * l2 + 1, 2 * l3 + 1), np.complex128)
        for m1 in range(-l1, l1 + 1):
            for m2 in range(-l2, l2 + 1):
                if abs(m1 + m2) <= l3:
                    c[l1 + m1, l2 + m2, l3 + m1 + m2] = cg(l1, m1, l2, m2, l3, m1 + m2)
        r = np.real(np.einsum("ij,kl,mn,ikn->jlm", basis(l1), basis(l2), np.conj(basis(l3).T), c))
        return (r / np.linalg.norm(r)).astype(np.float32)

    n0 = math.sqrt(1.0 / 64) / math.sqrt(10.0)
    n1 = math.sqrt(3.0 / 96) / math.sqrt(10.0)
    out = np.zeros((P, R2, 4), np.float32)
    w000, w011, w101, w110, w121 = w3j(0, 0, 0), w3j(0, 1, 1), w3j(1, 0, 1), w3j(1, 1, 0), w3j(1, 2, 1)
    for p in range(P):
        if p < 32:
            out[p, 0, 0] = w000[0, 0, 0] * n0
            for j in range(3):
                out[p, 1 + j, 1:] = w011[0, j, :] * n1
        else:
            i = (p - 32) % 3
            out[p, 0, 1:] = w101[i, 0, :] * n1
            for j in range(3):
                out[p, 1 + j, 0] = w110[i, j, 0] * n0
            for j in range(5):
                out[p, 4 + j, 1:] = w121[i, j, :] * n1
    return out


NODE_TILES = ROWS // P
NT = 2 * J
LAST = ITERS - 1
assert NODE_TILES == NT * ITERS and TILES % 2 == 0
HALF = TILES // 2
BAD_MAX = 1 << 23
SLOTS = 7
assert ITERS % SLOTS == 0 and 2 * SLOTS * NT * P <= EDGES
LOT = 28
LOT_W = (LOT + 2) * P
assert TILES % LOT == 0 and 12288 + 2 * LOT_W <= EDGES
W = D + 2
C_W1, C_W3, C_W4, C_END = 128, 160, 256, 352


def spherical_columns():
    full = spherical_constants()
    out = np.zeros((P, 7), np.float32)
    for p in range(P):
        if p < 32:
            assert all(abs(full[p, 1 + j, 1 + k]) < 1e-9 for j in range(3) for k in range(3) if j != k)
            out[p, 0] = full[p, 1, 1]
        else:
            i = (p - 32) % 3
            assert all(abs(full[p, 1 + j, 0]) < 1e-9 for j in range(3) if j != i)
            out[p, 1 + i] = full[p, 1 + i, 0]
            out[p, 4 + i] = 1.0
    return out


def spherical_pairs():
    full = spherical_constants()
    return {(i, k): [(j, float(full[32 + i, 4 + j, 1 + k])) for j in range(5)
                     if abs(full[32 + i, 4 + j, 1 + k]) > 1e-9] for i in range(3) for k in range(3)}


class Step:

    def __init__(self, value, par, half):
        self.value, self.par, self.half = value, par, half

    def plus(self, n):
        return Step(self.value + n, (self.par + n) % 2, self.half + (self.par + n) // 2)

    def at_least(self, n):
        return not isinstance(self.value, int) or self.value >= n


def number(n):
    return Step(n, n % 2, n // 2)


def build(nc, x, src, dst, dst_next, dst_flat, type8_flat, attr, type16, type8, w_rel, root, bias,
          self_w, bases, base_w,
          w0, w1, w2, w3, w4, w_msg, b_msg, w_att, b_att, w_ihT, b_ih, w_hhT, b_hh, gamma, beta,
          sph, sph_cols, out):
    with ExitStack() as ctx:
        def sb(name, *shape, dt=F32, keep=ctx):
            return keep.enter_context(nc.sbuf_tensor(name, list(shape), dt))

        phase_sems = []

        def sems(*names):
            new = [nc.alloc_semaphore(name=n) for n in names]
            phase_sems.extend(new)
            return new

        def end_phase():
            nc.clear_and_free_semaphores(phase_sems)
            phase_sems.clear()
            nc.all_engine_barrier()

        def table(name, rows, cols):
            return nc.dram_tensor(name, [rows, cols], F32, kind="Internal").ap()

        newT = table("newT", D, ROWS)

        passed = ctx.enter_context(nc.semaphore("passed"))

        def wait_apart(eng, sem, value):
            eng.wait_ge(sem, value)
            eng.sem_inc(passed, 1)

        def first(it):
            return isinstance(it, int) and it == 0

        ident = sb("ident", P, P)
        src_i, dst_i = sb("src_i", P, TILES, dt=I32), sb("dst_i", P, TILES, dt=I32)
        scat_i = sb("scat_i", P, TILES, dt=I32)
        src_now, dst_now = sb("src_now", P, 2, J, dt=I32), sb("dst_now", P, 2, J, dt=I32)
        scat_now = sb("scat_now", P, J, dt=I32)
        dst_f = sb("dst_f", P, TILES)
        wide = sb("wide", P, EDGES)
        dst_row = wide[:].bitcast(I32)
        dump_f = sb("dump_f", P, 1)
        repeat = sb("repeat", P, TILES)
        coef = sb("coef", P, TILES * R2)
        w_all = sb("w_all", P, R2 * P)
        b_row = sb("b_row", P, D)

        gx_flat, gd_flat = sb("gx", P, 2 * J * W), sb("gd", P, 2 * J * W)
        gx, gd = (t[:, 0:2 * J * D].rearrange("p (a j d) -> p a j d", a=2, j=J) for t in (gx_flat, gd_flat))
        hs = sb("hs", P, 2, J, D)
        hd = sb("hd", P, J, D)
        hT = sb("hT", P, GROUP)
        aT = sb("aT", P, GROUP)
        prod = sb("prod", P, 2, R2 * D)
        msg = sb("msg", P, J, D)
        comb = sb("comb", P, J, D)
        stats = sb("stats", P, 2 * J, 6)
        mv = sb("mv", P, 2 * J, 2)
        rstd, shift = sb("rstd", P, 2 * J), sb("shift", P, 2 * J)
        std = sb("std", P, 2 * J)
        att = sb("att", P, 3, J)
        psum = ctx.enter_context(nc.psum_tensor("psum", [P, 8, PB], F32))

        def pick_coefficients(eng, done, kind, types, picked):
            acc = coef[:, 0:TILES * R1].rearrange("p (t b) -> p t b", b=R1)
            eng.memset(coef[:, 0:TILES * R1], 0.0).then_inc(done, 1)
            eng.wait_ge(done, 1)
            n = 1
            for r in range(N_TYPE16):
                for b in range(R1):
                    w = types[:, r * R1 + b:r * R1 + b + 1]
                    eng.tensor_scalar(picked[:, :, b], kind, float(r), w, ALU.is_equal, ALU.mult).then_inc(done, 1)
                n += R1
                eng.wait_ge(done, n)
                for b in range(R1):
                    eng.tensor_tensor(acc[:, :, b], acc[:, :, b], picked[:, :, b], ALU.add).then_inc(done, 1)
                n += R1
                eng.wait_ge(done, n)

        def basis_coefficients(name, picked):
            ld1, c1 = sems(name + "_ld", name + "_step")
            with nc.Block() as block:
                kind, types = repeat[:].bitcast(I32), prod[:, 0, 0:N_TYPE16 * R1]

                @block.sync
                def _(sp):
                    sp.dma_start(kind, type16).then_inc(ld1, 16)
                    sp.dma_start(types, base_w.broadcast_to([P, N_TYPE16 * R1])).then_inc(ld1, 16)
                    sp.dma_start(w_all[:, 0:R1 * D].rearrange("p (b o) -> p b o", b=R1),
                                 bases.rearrange("b i o -> i b o")).then_inc(ld1, 16)
                    sp.wait_ge(ld1, 48)

                @block.vector
                def _(dve):
                    dve.wait_ge(ld1, 48)
                    pick_coefficients(dve, c1, kind, types, picked)
            end_phase()


        gate_w = sb("gate_w", P, 6 * D)
        wi, wh = gate_w[:, 0:3 * D], gate_w[:, 3 * D:6 * D]
        bvec = att[:].rearrange("p a b -> p (a b)")
        bn_st = coef[:, 0:GROUPS * 6].rearrange("p (g c) -> p g c", c=6)

        def last_phase(name, x3):
            (f_ld, v_s, sd_s, y_s, tr_s, res_s, *dma) = sems(
                *[f"{name}_{n}" for n in ("ld", "v", "sd", "y", "tr", "res")],
                *[f"{name}_{n}{a}" for n in ("ld", "st") for a in range(SLOTS)])
            loaded, stored = dma[:SLOTS], dma[SLOTS:]
            gb = att[:].rearrange("p a b -> p (a b)")
            step_w = NT * P
            slot = [wide[:, 2 * a * step_w:2 * (a + 1) * step_w] for a in range(SLOTS)]
            rows = [t[:, 0:step_w] for t in slot]
            updT = [t[:, step_w:2 * step_w] for t in slot]
            row_tile = lambda tab, g: tab[bass.ds(g * step_w, step_w), 0:D].rearrange(
                "(j p) d -> p j d", p=P)
            banks = lambda a: psum[:, 2 * (a % 3):2 * (a % 3) + 2, :]

            def laps(engine, body):
                for a in range(SLOTS):
                    body(a, a, 0)
                with engine.Fori(1, ITERS // SLOTS) as lap:
                    for a in range(SLOTS):
                        body(lap * SLOTS + a, a, lap)

            with nc.Block() as block:
                @block.sync
                def _(sp):
                    sp.dma_start(gb[:, 0:1], gamma).then_inc(f_ld, 16)
                    sp.dma_start(gb[:, 1:2], beta).then_inc(f_ld, 16)

                    def load(g, a, lap):
                        if not first(lap):
                            sp.wait_ge(stored[a], lap * 16)
                        sp.dma_start(updT[a], newT[:, bass.ds(g * step_w, step_w)]).then_inc(loaded[a], 16)
                        sp.dma_start(rows[a].rearrange("p (j d) -> p j d", d=D), row_tile(x3, g)
                                     ).then_inc(loaded[a], 16)
                    laps(sp, load)

                @block.scalar
                def _(act):
                    act.wait_ge(v_s, 2)
                    act.activation(std[:, 0:1], std[:, 0:1], ACT.Sqrt).then_inc(sd_s, 1)
                    act.wait_ge(v_s, 5)

                    def scaled(g, a, lap):
                        act.wait_ge(loaded[a], lap * 32 + 32)
                        act.activation(updT[a], updT[a], ACT.Identity, bias=gb[:, 3:4], scale=gb[:, 2:3]
                                       ).then_inc(y_s, 1)
                    laps(act, scaled)

                @block.tensor
                def _(pe):
                    def flip(g, a, lap):
                        pe.wait_ge(y_s, g + 1)
                        if not first(lap) or a >= 3:
                            pe.wait_ge(res_s, g if a == 0 else g - 2)
                        for k in range(NT):
                            mm = pe.transpose(banks(a)[:, k // J, k % J * P:(k % J + 1) * P],
                                              updT[a][:, k * P:(k + 1) * P], ident[:])
                        mm.then_inc(tr_s, 1)
                    laps(pe, flip)

                @block.vector
                def _(dve):
                    dve.wait_ge(f_ld, 32)
                    dve.bn_aggr(mv[:, 0, :], coef[:, 0:GROUPS * 6]).then_inc(v_s, 1)
                    dve.wait_ge(v_s, 1)
                    dve.tensor_scalar(std[:, 0:1], mv[:, 0, 1:2], EPS, None, ALU.add).then_inc(v_s, 1)
                    dve.wait_ge(sd_s, 1)
                    dve.reciprocal(rstd[:, 0:1], std[:, 0:1]).then_inc(v_s, 1)
                    dve.wait_ge(v_s, 3)
                    dve.tensor_tensor(gb[:, 2:3], rstd[:, 0:1], gb[:, 0:1], ALU.mult).then_inc(v_s, 1)
                    dve.wait_ge(v_s, 4)
                    dve.scalar_tensor_tensor(out=shift[:, 0:1], in0=mv[:, 0, 0:1], scalar=-1.0,
                                             in1=gb[:, 2:3], op0=ALU.mult, op1=ALU.mult).then_inc(f_ld, 1)
                    dve.wait_ge(f_ld, 33)
                    dve.tensor_tensor(gb[:, 3:4], gb[:, 1:2], shift[:, 0:1], ALU.add).then_inc(v_s, 1)

                    def add(g, a, lap):
                        dve.wait_ge(loaded[a], lap * 32 + 32)
                        dve.wait_ge(tr_s, g + 1)
                        dve.tensor_tensor(rows[a], banks(a).rearrange("p b q -> p (b q)"), rows[a],
                                          ALU.add).then_inc(res_s, 1)
                    laps(dve, add)

                @block.gpsimd
                def _(pool):
                    def store(g, a, lap):
                        wait_apart(pool, res_s, g + 1)
                        pool.dma_start(row_tile(out, g), rows[a].rearrange("p (j d) -> p j d", d=D)
                                       ).then_inc(stored[a], 16)
                    laps(pool, store)
                    for q in stored:
                        pool.wait_ge(q, 16 * (ITERS // SLOTS))
            end_phase()

        ld, const, conv = sems("set_ld", "set_const", "set_conv")
        with nc.Block() as block:
            @block.sync
            def _(sp):
                sp.dma_start(src_i[:], src).then_inc(ld, 16)
                sp.dma_start(dst_i[:], dst).then_inc(ld, 16)
                sp.dma_start(b_row[:], bias.broadcast_to([P, D])).then_inc(ld, 16)
                sp.wait_ge(ld, 48)

            @block.gpsimd
            def _(pool):
                pool.memset(ident[:], 0.0).then_inc(const, 1)
                pool.wait_ge(const, 1)
                pool.affine_select(out=ident[:], in_=ident[:], compare_op=ALU.not_equal, fill=1.0,
                                   base=0, pattern=[[-1, P]], channel_multiplier=1).then_inc(const, 1)

            @block.vector
            def _(dve):
                dve.wait_ge(ld, 48)
                dve.tensor_copy(dst_f[:], dst_i[:]).then_inc(conv, 1)
                dve.wait_ge(conv, 1)
        end_phase()

        window_i = sb("window_i", 1, NODE_TILES, dt=I32)
        bad_i = sb("bad_i", 1, 1, dt=I32)
        ids = sb("ids", P, P)
        rel = sb("rel", P, NODE_TILES, 2)
        ones = sb("ones", P, P)
        rel_flat = rel[:].rearrange("p n w -> p (n w)")

        ld, const, step, picked, pe_done = sems("plan_ld", "plan_const", "plan_step", "plan_pick", "plan_pe")
        with nc.Block() as block:
            ends_i = scat_i[0:HALF, 0:2]
            ends = std[0:HALF, 0:2]
            starts = wide[:, 0:NODE_TILES]
            limit = wide[:, 512:512 + NODE_TILES]
            later = [wide[0:HALF, 1024 + 512 * c:1024 + 512 * c + NODE_TILES] for c in range(2)]
            diag = [wide[0:HALF, 2048 + 128 * c:2048 + 128 * c + HALF] for c in range(2)]
            window = wide[:, 2560:2560 + NODE_TILES]
            next_i = wide[:, 3072:3072 + TILES].bitcast(I32)
            next_f = wide[:, 3328:3328 + TILES]
            floor_i = wide[:, 3584:3584 + TILES].bitcast(I32)
            floor_f = wide[:, 3840:3840 + TILES]
            flags = wide[:, 4096:4096 + 1024]
            viol = wide[:, 5120:5121]
            minus_base = wide[:, 5632:5632 + NODE_TILES]
            by_edge_i = wide[0:HALF, 6144:6144 + 2 * P].bitcast(I32)
            by_edge = wide[0:HALF, 6656:6656 + 2 * P]
            tile_no = wide[0:HALF, 7168:7172]
            pick = [wide[0:HALF, 7680 + 512 * q:7680 + 512 * q + NODE_TILES] for q in range(4)]

            @block.sync
            def _(sp):
                ends_dram = dst_flat.rearrange("a (c p q) -> p c (a q)", c=2, p=HALF)[:, :, P - 1:P]
                with nc.allow_non_contiguous_dma(reason="one word for each edge tile"):
                    sp.dma_start(ends_i, ends_dram.rearrange("p c q -> p (c q)")).then_inc(ld, 16)
                sp.dma_start(next_i, dst_next).then_inc(ld, 16)
                sp.dma_start(by_edge_i, dst_flat.rearrange("a (c p q) -> p c (a q)", c=2, p=HALF)).then_inc(ld, 16)
                sp.wait_ge(ld, 48)

            @block.gpsimd
            def _(pool):
                imprecise = dict(allow_small_or_imprecise_dtypes=True)
                pool.iota(ids[:], [[1, P]], base=0, channel_multiplier=0, **imprecise).then_inc(const, 1)
                pool.iota(starts, [[P, NODE_TILES]], base=0, channel_multiplier=0, **imprecise).then_inc(const, 1)
                pool.iota(minus_base, [[-P, NODE_TILES]], base=0, channel_multiplier=0,
                          **imprecise).then_inc(const, 1)
                pool.iota(limit, [[J, ITERS], [0, NT]], base=2 * J - 2, channel_multiplier=0,
                          **imprecise).then_inc(const, 1)
                pool.memset(ones[:], 1.0).then_inc(const, 1)
                pool.memset(flags, 0.0).then_inc(const, 1)
                pool.iota(tile_no, [[HALF, 2], [-1, 2]], base=0, channel_multiplier=1,
                          **imprecise).then_inc(const, 1)

            @block.vector
            def _(dve):
                dve.wait_ge(ld, 48)
                dve.wait_ge(const, 7)
                dve.tensor_copy(by_edge, by_edge_i).then_inc(picked, 1)
                dve.tensor_copy(ends, ends_i).then_inc(step, 1)
                dve.tensor_copy(next_f, next_i).then_inc(step, 1)
                dve.tensor_scalar(floor_i, dst_i[:], 7, 7, ALU.logical_shift_right,
                                  ALU.logical_shift_left).then_inc(step, 1)
                dve.wait_ge(step, 3)
                dve.tensor_copy(floor_f, floor_i).then_inc(step, 1)
                for c in range(2):
                    dve.tensor_scalar(later[c], starts[0:HALF, :], ends[:, c:c + 1], None,
                                      ALU.is_gt).then_inc(step, 1)
                    dve.tensor_scalar(diag[c], ident[0:HALF, 0:HALF], ends[:, c:c + 1], None,
                                      ALU.mult).then_inc(step, 1)
                dve.wait_ge(pe_done, 1)
                dve.wait_ge(step, 8)
                dve.tensor_tensor(flags[:, 0:TILES], dst_f[:], next_f, ALU.is_gt).then_inc(step, 1)
                dve.tensor_tensor(flags[:, TILES:2 * TILES - 2], psum[:, 1, 0:TILES - 2], floor_f[:, 2:TILES],
                                  ALU.is_ge).then_inc(step, 1)
                dve.tensor_scalar(window, psum[:, 0, 0:NODE_TILES], float(TILES - 2), None,
                                  ALU.min).then_inc(step, 1)
                dve.wait_ge(step, 11)
                dve.tensor_tensor(flags[:, 512:512 + NODE_TILES], window, limit, ALU.is_gt).then_inc(step, 1)
                dve.tensor_copy(window_i[:], window[0:1, :]).then_inc(step, 1)
                dve.wait_ge(step, 13)
                dve.tensor_reduce(viol, flags, AX_X, ALU.add).then_inc(step, 1)
                dve.wait_ge(pe_done, 2)
                dve.tensor_copy(bad_i[:], psum[0:1, 2, 0:1]).then_inc(step, 1)
                dve.wait_ge(step, 15)
                for q in range(4):
                    dve.tensor_scalar(pick[q], window[0:HALF, :], tile_no[:, q:q + 1], None,
                                      ALU.is_equal).then_inc(picked, 1)
                dve.wait_ge(pe_done, 3)
                for w in range(2):
                    dve.tensor_tensor(rel[:, :, w], psum[:, 3 + w, 0:NODE_TILES], minus_base,
                                      ALU.add).then_inc(step, 1)
                dve.wait_ge(step, 17)

            @block.tensor
            def _(pe):
                pe.wait_ge(const, 6)
                pe.wait_ge(step, 8)
                for c in range(2):
                    pe.matmul(psum[:, 0, 0:NODE_TILES], ones[0:HALF, :], later[c], start=c == 0, stop=c == 1)
                for c in range(2):
                    mm = pe.matmul(psum[:, 1, c * HALF:(c + 1) * HALF], ones[0:HALF, :], diag[c],
                                   start=True, stop=True)
                mm.then_inc(pe_done, 1)
                pe.wait_ge(step, 14)
                pe.matmul(psum[:, 2, 0:1], ones[:], viol, start=True, stop=True).then_inc(pe_done, 1)
                pe.wait_ge(picked, 5)
                for w in range(2):
                    for c in range(2):
                        mm = pe.matmul(psum[:, 3 + w, 0:NODE_TILES], by_edge[:, c * P:(c + 1) * P],
                                       pick[2 * c + w], start=c == 0, stop=c == 1)
                mm.then_inc(pe_done, 1)
        end_phase()

        def sorted_program(own):
            key_pad = nc.dram_tensor("key_pad", [1, EDGES + 2 * P], F32, kind="Internal").ap()
            messages = wide[:]

            def own_sb(name, *shape):
                return sb(name, *shape, keep=own)

            x1, x2, x3 = table("x1_w", ROWS, W), table("x2_w", ROWS, W), table("x3_w", ROWS, W)
            nx, nh = own_sb("nx", P, 2, NT, W), own_sb("nh", P, NT, D)
            gxw, gdw = (t[:].rearrange("p (a j d) -> p a j d", a=2, j=J) for t in (gx_flat, gd_flat))
            xb = [gd[:].rearrange("p a j d -> p (a j) d"),
                  prod[:].rearrange("p a q -> p (a q)")[:, 2 * GROUP:2 * GROUP + NT * D]
                  .rearrange("p (j d) -> p j d", j=NT)]
            nhT = own_sb("nhT", P, 2, GROUP)
            res = own_sb("res", P, 2, NT, W)
            newT_now = res[:].rearrange("p a j d -> p a (j d)")[:, :, 0:NT * P]
            sel = own_sb("sel", P, 2, 2 * J, P)
            rel_now = own_sb("rel_now", P, 2, 2 * J)
            masked = own_sb("masked", P, R0, GROUP)
            prod_flat = prod[:].rearrange("p a q -> p (a q)")
            kinds = prod_flat[:, 0:2 * GROUP].bitcast(I32).rearrange("p (a q) -> p a q", a=2)
            invcnt = own_sb("invcnt", P, TILES)
            st_of, mv_of, sd_of, rs_of, sh_of = {}, {}, {}, {}, {}
            for q in "eno":
                st_of[q], mv_of[q] = own_sb(q + "_st", P, 2, NT, 6), own_sb(q + "_mv", P, 2, NT, 2)
                sd_of[q] = own_sb(q + "_sd", P, 2, NT)
                if q == "o":
                    rs_of[q], sh_of[q] = res[:, :, :, D], res[:, :, :, D + 1]
                else:
                    rs_of[q], sh_of[q] = own_sb(q + "_rs", P, 2, NT), own_sb(q + "_sh", P, 2, NT)
            e_rs, e_sh, n_rs, n_sh = rs_of["e"], sh_of["e"], rs_of["n"], sh_of["n"]
            mix = masked[:].rearrange("p r q -> p (r q)")[:, 0:TILES * 9]
            att_s = own_sb("att_s", P, 2, 3, J)

            ld, ld16, coef_s, st, step, tr_s, k0, k1, dn = sems("key_ld", "key_ld16", "key_coef", "key_st", "key_step", "key_tr",
                                                         "key_k0", "key_k1", "key_dn")
            with nc.Block() as block:
                kind_i = wide[:, 0:TILES].bitcast(I32)
                key = wide[:, 512:512 + TILES]
                flipped = wide[0:HALF, 1024:1024 + 2 * P]
                rows = [wide[:, 12288 + LOT_W * a:12288 + LOT_W * (a + 1)] for a in range(2)]
                equal = [wide[:, 4096 + 3 * P * q:4096 + 3 * P * (q + 1)] for q in range(LOT // 4)]
                kind16, types, picked = (wide[:, 8704:8704 + TILES].bitcast(I32), wide[:, 9216:9216 + N_TYPE16 * R1],
                                         wide[:, 9728:9728 + TILES * R1].rearrange("p (t b) -> p t b", b=R1))
                none = wide[0:1, 8192:8192 + P]

                @block.sync
                def _(sp):
                    sp.dma_start(kind_i, type8).then_inc(ld, 16)
                    sp.dma_start(kind16, type16).then_inc(ld16, 16)
                    sp.dma_start(types, base_w.broadcast_to([P, N_TYPE16 * R1])).then_inc(ld16, 16)
                    sp.wait_ge(step, 1)
                    sp.dma_start(key_pad[:, 0:P], none).then_inc(st, 16)
                    sp.dma_start(key_pad[:, P + EDGES:2 * P + EDGES], none).then_inc(st, 16)
                    sp.wait_ge(step, 4)
                    for c in range(2):
                        at = P + c * HALF * P
                        sp.dma_start(key_pad[:, at:at + HALF * P].rearrange("a (p q) -> p (a q)", q=P),
                                     flipped[:, c * P:(c + 1) * P]).then_inc(st, 16)
                    sp.wait_ge(st, 64)

                    for lot in range(TILES // LOT):
                        if lot >= 2:
                            sp.wait_ge(dn, (lot - 1) * LOT)
                        sp.dma_start(rows[lot % 2], key_pad[:, lot * LOT * P:lot * LOT * P + LOT_W]
                                     .broadcast_to([P, LOT_W])).then_inc((k0, k1)[lot % 2], 16)

                @block.gpsimd
                def _(pool):
                    pool.wait_ge(ld16, 32)
                    pick_coefficients(pool, coef_s, kind16, types, picked)

                @block.tensor
                def _(pe):
                    pe.wait_ge(step, 3)
                    for c in range(2):
                        mm = pe.transpose(psum[0:HALF, 0, c * P:(c + 1) * P], key[:, c * HALF:(c + 1) * HALF],
                                          ident[:])
                    mm.then_inc(tr_s, 1)

                @block.vector
                def _(dve):
                    dve.memset(none, -1.0).then_inc(step, 1)
                    dve.wait_ge(ld, 16)
                    dve.tensor_copy(invcnt[:], kind_i).then_inc(step, 1)
                    dve.wait_ge(step, 2)
                    dve.scalar_tensor_tensor(out=key, in0=dst_f[:], scalar=float(R0), in1=invcnt[:],
                                             op0=ALU.mult, op1=ALU.add).then_inc(step, 1)
                    dve.wait_ge(tr_s, 1)
                    dve.tensor_copy(flipped, psum[0:HALF, 0, 0:2 * P]).then_inc(step, 1)

                    for lot in range(TILES // LOT):
                        dve.wait_ge((k0, k1)[lot % 2], lot // 2 * 16 + 16)
                        with dve.Fori(0, 4) as quarter:
                            for q in range(LOT // 4):
                                k = quarter * (LOT // 4) + q
                                dve.tensor_scalar(equal[q], rows[lot % 2][:, bass.ds(k * P, 3 * P)],
                                                  key[:, bass.ds(k + lot * LOT, 1)], 0.0, ALU.is_equal, ALU.add,
                                                  accum_out=invcnt[:, bass.ds(k + lot * LOT, 1)]).then_inc(dn, 1)
                            dve.wait_ge(dn, quarter * (LOT // 4) + (lot * LOT + LOT // 4))
                    dve.reciprocal(invcnt[:], invcnt[:]).then_inc(step, 1)
                    dve.wait_ge(step, 5)
            end_phase()

            def steps(body):
                def run(engine):
                    for i in range(3):
                        body(number(i))
                    with engine.Fori(1, (ITERS - 5) // 2) as m:
                        body(Step(m * 2 + 1, 1, m))
                        body(Step(m * 2 + 2, 0, m + 1))
                    for i in range(ITERS - 4, ITERS):
                        body(number(i))
                return run

            def has(i, ahead):
                return not isinstance(i.value, int) or i.value + ahead <= LAST

            def load_windows(i, engine):
                return nc.values_load_multi_w_load_instructions(
                    window_i[0:1, bass.ds(i.value * NT, NT)], engines=(engine,),
                    min_val=0, max_val=TILES - 2,
                    skip_runtime_bounds_check_because="the windows are clipped when they are made")[1]

            def selections(eng, sel_made, sums_done, i, c, copied=None):
                if i.at_least(1):
                    wait_apart(eng, sums_done, i.value * 2 + (c - 1))
                if copied is not None:
                    eng.tensor_copy(rel_now[:, c, :], rel_flat[:, bass.ds(i.value * 2 * NT + c * 2 * J, 2 * J)]
                                    ).then_inc(copied[c], 1)
                    wait_apart(eng, copied[c], i.value + 1)
                    for w in range(2 * J):
                        ins = eng.tensor_scalar(sel[:, c, w, :], ids[:], rel_now[:, c, w:w + 1], None,
                                                ALU.is_equal)
                    ins.then_inc(sel_made[c], 1)
                    return
                eng.tensor_tensor(sel[:, c], ids[:].rearrange("p (o q) -> p o q", o=1)
                                  .broadcast_to([P, 2 * J, P]),
                                  rel_flat[:, bass.ds(i.value * 2 * NT + c * 2 * J, 2 * J)]
                                  .rearrange("p (w o) -> p w o", o=1).broadcast_to([P, 2 * J, P]),
                                  ALU.is_equal).then_inc(sel_made[c], 1)

            def ready(pe, messages_made, sel_made, i, c):
                pe.wait_ge(messages_made, i.value * J + 2 * J if has(i, 1) else TILES)
                pe.wait_ge(sel_made[c], i.value + 1)

            def sums(pe, i, c, windows, bank, node_w):
                for j in range(J):
                    o = psum[:, bank, j * D:(j + 1) * D]
                    if node_w is not None:
                        pe.matmul(o, nhT[:, c, j * P:(j + 1) * P], node_w, start=True, stop=False)
                    for w in range(2):
                        mm = pe.matmul(o, sel[:, c, 2 * j + w, :],
                                       messages[:, bass.ds(windows[c * J + j] * D + w * D, D)],
                                       start=node_w is None and w == 0, stop=w == 1)
                return mm

            def fused(name, kind, x_in, x_out, weights, node_weight=None):
                dense = kind == 0 or kind == 1
                names = ["w", "ga0", "ga1", "nl0", "nl1", "st0", "st1", "kl0", "kl1", "index",
                         "e_stat", "e_mv", "e_var", "e_std", "e_rs", "e_sh",
                         "n_stat", "n_mv", "n_var", "n_std", "n_rs", "n_sh",
                         "o_stat", "o_mv", "o_var", "o_std", "o_rs", "o_sh",
                         "eh", "etr", "eev", "emask", "emm", "part", "msg", "nh", "ntr", "nev", "sel0", "sel1",
                         "rel0", "rel1",
                         "ndone", "res", "xb", "mul", "zero"]
                s = dict(zip(names, sems(*[f"{name}_{n}" for n in names])))
                sel_on_dve = (0, 1) if kind == 1 else (1,)
                ga, nl, st, kl, sel_made = ([s[f"{q}{a}"] for a in range(2)] for q in ("ga", "nl", "st", "kl", "sel"))
                node_w = w_all[:, R0 * P:(R0 + 1) * P]
                n_w = len(weights) + (node_weight is not None)
                xin_w = D if kind == 0 else W
                gx_, nx_ = gxw[:, :, :, 0:xin_w], nx[:, :, :, 0:xin_w]
                row_tile = lambda tab, i: tab[bass.ds(i.value * (NT * P), NT * P), :].rearrange(
                    "(j p) d -> p j d", p=P)

                def stats_half(dve, which, n, q, tiles):
                    a = q.par
                    for k in range(n):
                        dve.bn_stats(st_of[which][:, a, k, :], tiles(k)).then_inc(s[which + "_stat"], 1)
                    wait_apart(dve, s[which + "_stat"], q.value * n + n)
                    for k in range(n):
                        dve.bn_aggr(mv_of[which][:, a, k, :], st_of[which][:, a, k, :]
                                    ).then_inc(s[which + "_mv"], 1)
                    dve.wait_ge(s[which + "_mv"], q.value * n + n)
                    dve.tensor_scalar(sd_of[which][:, a, 0:n], mv_of[which][:, a, 0:n, 1], EPS, None,
                                      ALU.add).then_inc(s[which + "_var"], 1)

                def root_half(act, which, n, q):
                    act.wait_ge(s[which + "_var"], q.value + 1)
                    act.activation(sd_of[which][:, q.par, 0:n], sd_of[which][:, q.par, 0:n],
                                   ACT.Sqrt).then_inc(s[which + "_std"], 1)

                def scale_half(dve, which, n, q):
                    a = q.par
                    dve.wait_ge(s[which + "_std"], q.value + 1)
                    dve.reciprocal(rs_of[which][:, a, 0:n], sd_of[which][:, a, 0:n]).then_inc(s[which + "_rs"], 1)
                    dve.wait_ge(s[which + "_rs"], q.value + 1)
                    dve.scalar_tensor_tensor(out=sh_of[which][:, a, 0:n], in0=mv_of[which][:, a, 0:n, 0],
                                             scalar=-1.0, in1=rs_of[which][:, a, 0:n], op0=ALU.mult,
                                             op1=ALU.mult).then_inc(s[which + "_sh"], 1)

                def pool_program(pool):
                    def gather(e):
                        a = e.par
                        if e.at_least(2):
                            wait_apart(pool, s["eh"], e.value * J - J)
                        pool.tensor_copy(src_now[:, a, :], src_i[:, bass.ds(e.value * J, J)]).then_inc(s["index"], 1)
                        wait_apart(pool, s["index"], e.value + 1)
                        for k in range(J):
                            pool.indirect_dma_start(gx_[:, a, k, :], None, x_in,
                                                    bass.IndirectOffsetOnAxis(src_now[:, a, k:k + 1], 0)
                                                    ).then_inc(ga[a], 16)

                    copied = (s["rel0"], s["rel1"])

                    def keep_rows(i):
                        if dense:
                            wait_apart(pool, nl[i.par], i.half * 16 + 16)
                            if i.at_least(2):
                                wait_apart(pool, s["res"], i.value * 2 - 2)
                            if kind == 1:
                                pool.tensor_copy(xb[i.par], nx_[:, i.par, :, 0:D]).then_inc(s["xb"], 1)
                                return
                            pool.tensor_tensor(xb[i.par], nx_[:, i.par], b_row[:].rearrange("p (o d) -> p o d", o=1)
                                               .broadcast_to([P, NT, D]), ALU.add).then_inc(s["xb"], 1)

                    for e in range(4):
                        gather(number(e))
                    keep_rows(number(0))
                    sel_on_pool = [c for c in range(2) if c not in sel_on_dve]
                    for c in sel_on_pool:
                        selections(pool, sel_made, s["ndone"], number(0), c, copied)

                    def body(i):
                        if has(i, 4):
                            gather(i.plus(4))
                        if 0 in sel_on_pool and has(i, 1):
                            selections(pool, sel_made, s["ndone"], i.plus(1), 0, copied)
                        if has(i, 1):
                            keep_rows(i.plus(1))
                        if 1 in sel_on_pool and has(i, 1):
                            selections(pool, sel_made, s["ndone"], i.plus(1), 1, copied)
                    steps(body)(pool)

                def sp_program(sp):
                    for dst_ap, src_ap in weights:
                        sp.dma_start(dst_ap, src_ap).then_inc(s["w"], 16)
                    if node_weight is not None:
                        sp.dma_start(node_w, node_weight).then_inc(s["w"], 16)

                    def load_kinds(e):
                        if kind == 0:
                            if e.at_least(2):
                                sp.wait_ge(s["emask"], e.value * R0 - R0)
                            sp.dma_start(kinds[:, e.par, :], type8_flat[:, bass.ds(e.value * GROUP, GROUP)]
                                         .broadcast_to([P, GROUP])).then_inc(kl[e.par], 16)

                    def load_nodes(i):
                        if i.at_least(2) and dense:
                            wait_apart(sp, s["nh"], i.value * NT - NT)
                            wait_apart(sp, s["xb"], i.value - 1)
                        elif i.at_least(2):
                            sp.wait_ge(s["res"], i.value * 2 - 2)
                        sp.dma_start(nx_[:, i.par], row_tile(x_in, i)).then_inc(nl[i.par], 16)

                    def store(i):
                        sp.wait_ge(s["o_sh"], i.value + 1)
                        sp.dma_start(row_tile(x_out, i), res[:, i.par]).then_inc(st[i.par], 16)

                    for e in range(2):
                        load_kinds(number(e))
                        load_nodes(number(e))
                    load_kinds(number(2))
                    load_kinds(number(3))

                    def body(i):
                        if has(i, 4):
                            load_kinds(i.plus(4))
                        if has(i, 2):
                            load_nodes(i.plus(2))
                        if i.at_least(1):
                            store(i.plus(-1))
                    steps(body)(sp)
                    store(number(LAST))
                    sp.wait_ge(st[0], 16 * (LAST // 2 + 1))
                    sp.wait_ge(st[1], 16 * ((LAST + 1) // 2))

                def act_program(act):
                    def edge_relu(e):
                        a = e.par
                        if kind == 0:
                            act.wait_ge(s["e_sh"], e.value + 1)
                        else:
                            act.wait_ge(ga[a], e.half * 16 * J + 16 * J)
                        if e.at_least(2):
                            act.wait_ge(s["etr"], e.value - 1)
                        for k in range(J):
                            rs, sh = ((e_rs[:, a, k:k + 1], e_sh[:, a, k:k + 1]) if kind == 0 else
                                      (gx_[:, a, k, D:D + 1], gx_[:, a, k, D + 1:D + 2]))
                            act.activation(hs[:, a, k, :], gx_[:, a, k, 0:D], ACT.Relu, bias=sh,
                                           scale=rs).then_inc(s["eh"], 1)

                    def edge_messages(e):
                        for k in range(J):
                            t = e.value * J + k
                            if kind in (0, 1) and k == 0:
                                act.wait_ge(s["emm"], e.value * J + J)
                            if kind == 0:
                                act.activation(messages[:, bass.ds(t * D, D)], psum[:, 1, k * D:(k + 1) * D],
                                               ACT.Copy, scale=invcnt[:, bass.ds(t, 1)]).then_inc(s["msg"], 1)
                            elif kind == 1:
                                if k == 0 and e.at_least(1):
                                    act.wait_ge(s["msg"], e.value * J)
                                act.activation(prod[:, 0, k * D:(k + 1) * D],
                                               psum[:, 1, k * D:(k + 1) * D],
                                               ACT.Copy, scale=coef[:, bass.ds(t * R1, 1)]).then_inc(s["part"], 1)
                            else:
                                act.wait_ge(s["emm"], t + 1)
                                if k == 3 or e.at_least(1):
                                    act.wait_ge(s["msg"], e.value * J + (0, -2, -1, 1)[k])
                                b, z = psum[:, (1, 4)[k % 2], :], product(k)
                                for c in range(3):
                                    act.activation(z[:, 32 + c:D:3, 3], b[:, C_W1:C_W3], ACT.Copy,
                                                   scale=coef[:, bass.ds(t * R2 + (1 + c), 1)])
                                act.activation(z[:, :, 4], b[:, 0:D], ACT.Copy,
                                               scale=coef[:, bass.ds(t * R2, 1)]).then_inc(s["part"], 1)

                    def node_relu(i):
                        if kind == 0:
                            act.wait_ge(s["n_sh"], i.value + 1)
                        else:
                            act.wait_ge(nl[i.par], i.half * 16 + 16)
                        if i.at_least(1):
                            act.wait_ge(s["ntr"], i.value * 2)
                        for k in range(NT):
                            rs, sh = ((n_rs[:, i.par, k:k + 1], n_sh[:, i.par, k:k + 1]) if kind == 0 else
                                      (nx_[:, i.par, k, D:D + 1], nx_[:, i.par, k, D + 1:D + 2]))
                            act.activation(nh[:, k, :], nx_[:, i.par, k, 0:D], ACT.Relu, bias=sh,
                                           scale=rs).then_inc(s["nh"], 1)

                    def node_evacuate(i, c):
                        act.wait_ge(s["ntr"], i.value * 2 + (c + 1))
                        if i.at_least(1):
                            act.wait_ge(s["ndone"], i.value * 2 + (c - 1))
                        act.activation(nhT[:, c, :], psum[:, 3 + c, :], ACT.Copy).then_inc(s["nev"], 1)

                    def next_relus(i):
                        if has(i, 3):
                            edge_relu(i.plus(3))
                        if dense and has(i, 1):
                            node_relu(i.plus(1))

                    def next_roots(i):
                        if kind == 0 and has(i, 2):
                            root_half(act, "n", NT, i.plus(2))
                        if kind == 0 and has(i, 4):
                            root_half(act, "e", J, i.plus(4))

                    def edge_evacuate(e):
                        if kind == 2:
                            act.wait_ge(s["etr"], e.value + 1)
                            if e.at_least(1):
                                act.wait_ge(s["emm"], e.value * J)
                            act.activation(hT[:], psum[:, 0, :], ACT.Copy).then_inc(s["eev"], 1)

                    if kind == 2:
                        act.wait_ge(s["zero"], 1)
                    for e in (number(0), number(1)):
                        if kind == 0:
                            root_half(act, "e", J, e)
                        edge_relu(e)
                        edge_evacuate(e)
                        edge_messages(e)
                    next_roots(number(-2))
                    next_relus(number(-1))
                    next_roots(number(-1))
                    edge_evacuate(number(2))
                    if dense:
                        node_evacuate(number(0), 0)
                        node_evacuate(number(0), 1)
                    if kind == 2:
                        next_relus(number(0))

                    def body(i):
                        if kind == 2:
                            if has(i, 2):
                                edge_messages(i.plus(2))
                            if has(i, 3):
                                edge_evacuate(i.plus(3))
                            if i.at_least(1):
                                root_half(act, "o", NT, i.plus(-1))
                            if has(i, 4):
                                edge_relu(i.plus(4))
                            return
                        next_relus(i)
                        if has(i, 2):
                            edge_messages(i.plus(2))
                        if i.at_least(1):
                            root_half(act, "o", NT, i.plus(-1))
                        if has(i, 1):
                            node_evacuate(i.plus(1), 0)
                        next_roots(i)
                        if has(i, 1):
                            node_evacuate(i.plus(1), 1)
                    steps(body)(act)
                    root_half(act, "o", NT, number(LAST))

                def product(k):
                    return prod_flat[:, k % 3 * 5 * D:(k % 3 + 1) * 5 * D].rearrange("p (o c) -> p o c", c=5)

                def dve_program(dve):
                    def bring_hT(e):
                        if kind == 2:
                            return
                        dve.wait_ge(s["etr"], e.value + 1)
                        if e.at_least(1):
                            dve.wait_ge(s["emm"], e.value * J)
                        if kind == 0:
                            dve.wait_ge(kl[e.par], e.half * 16 + 16)
                            for r in range(R0):
                                dve.scalar_tensor_tensor(out=masked[:, r, :], in0=kinds[:, e.par, :],
                                                         scalar=float(r), in1=psum[:, 0, :], op0=ALU.is_equal,
                                                         op1=ALU.mult).then_inc(s["emask"], 1)
                        else:
                            dve.tensor_copy(hT[:], psum[:, 0, :]).then_inc(s["eev"], 1)

                    def edge_messages(e):
                        for k in range(J):
                            t = e.value * J + k
                            out = messages[:, bass.ds(t * D, D)]
                            if kind == 1:
                                dve.wait_ge(s["part"], t + 1)
                                if k == 0:
                                    dve.wait_ge(s["part"], e.value * J + J)
                                dve.scalar_tensor_tensor(out=out, in0=psum[:, 2, k * D:(k + 1) * D],
                                                         scalar=coef[:, bass.ds(t * R1 + 1, 1)],
                                                         in1=prod[:, 0, k * D:(k + 1) * D],
                                                         op0=ALU.mult, op1=ALU.add).then_inc(s["msg"], 1)
                                continue
                            dve.wait_ge(s["emm"], t + 1)
                            if k == 3 or e.at_least(1):
                                dve.wait_ge(s["msg"], e.value * J + (0, -2, -1, 1)[k])
                            z, b = product(k), psum[:, 2 + k % 2, :]
                            y1 = coef[:, bass.ds(t * R2 + 1, 3)].rearrange("p (o k) -> p o k", o=1)
                            m = mix[:, bass.ds(t * 9, 9)].rearrange("p (o k i) -> p o k i", o=1, k=3)
                            dve.tensor_tensor(z[:, 0:32, 0:3],
                                              b[:, C_W3:C_W4].rearrange("p (w i) -> p w i", i=3),
                                              y1.broadcast_to([P, 32, 3]), ALU.mult).then_inc(s["mul"], 1)
                            dve.tensor_tensor(z[:, 32:D, 0:3].rearrange("p (w k) i -> p w k i", k=3),
                                              b[:, C_W4:C_END].rearrange("p (w o i) -> p w o i", o=1, i=3)
                                              .broadcast_to([P, 32, 3, 3]),
                                              m.broadcast_to([P, 32, 3, 3]), ALU.mult).then_inc(s["mul"], 1)
                            if k > 0:
                                add_up(e, k - 1)
                        if kind == 2:
                            add_up(e, J - 1)

                    def add_up(e, k):
                        t = e.value * J + k
                        dve.wait_ge(s["part"], t + 1)
                        dve.wait_ge(s["mul"], t * 2 + 2)
                        dve.tensor_reduce(messages[:, bass.ds(t * D, D)], product(k), AX_X,
                                          ALU.add).then_inc(s["msg"], 1)

                    def residual(i, c):
                        if c == 0:
                            if dense:
                                dve.wait_ge(s["xb"], i.value + 1)
                            else:
                                dve.wait_ge(nl[i.par], i.half * 16 + 16)
                            if i.at_least(2):
                                dve.wait_ge(st[i.par], i.half * 16)
                        dve.wait_ge(s["ndone"], i.value * 2 + (c + 1))
                        base = xb[i.par][:, c * J:(c + 1) * J] if dense else nx_[:, i.par, c * J:(c + 1) * J, 0:D]
                        dve.tensor_tensor(res[:, i.par, c * J:(c + 1) * J, 0:D],
                                          psum[:, 5 + c, :].rearrange("p (j d) -> p j d", j=J),
                                          base, ALU.add).then_inc(s["res"], 1)

                    def next_stats(i):
                        if has(i, 2):
                            q = i.plus(2)
                            dve.wait_ge(nl[q.par], q.half * 16 + 16)
                            stats_half(dve, "n", NT, q, lambda k: nx_[:, q.par, k, :])
                        if has(i, 4):
                            e = i.plus(4)
                            dve.wait_ge(ga[e.par], e.half * 16 * J + 16 * J)
                            stats_half(dve, "e", J, e, lambda k: gx_[:, e.par, k, :])

                    def next_scales(i):
                        if has(i, 4):
                            scale_half(dve, "e", J, i.plus(4))
                        if has(i, 2):
                            scale_half(dve, "n", NT, i.plus(2))

                    if n_w:
                        dve.wait_ge(s["w"], 16 * n_w)
                    if kind == 2:
                        dve.memset(prod[:], 0.0).then_inc(s["zero"], 1)
                        dve.wait_ge(s["zero"], 1)
                    for e in (number(0), number(1)):
                        if kind == 0:
                            dve.wait_ge(ga[e.par], 16 * J)
                            stats_half(dve, "e", J, e, lambda k: gx_[:, e.par, k, :])
                            scale_half(dve, "e", J, e)
                        bring_hT(e)
                        if kind != 0:
                            edge_messages(e)
                    if kind == 0:
                        for i in (number(-2), number(-1)):
                            next_stats(i)
                            next_scales(i)
                    bring_hT(number(2))
                    for c in sel_on_dve:
                        selections(dve, sel_made, s["ndone"], number(0), c)

                    def result_stats(i):
                        wait_apart(dve, s["res"], i.value * 2 + 2)
                        stats_half(dve, "o", NT, i, lambda k: res[:, i.par, k, 0:D])

                    def finish(i, c):
                        residual(i, c)
                        if c in sel_on_dve and has(i, 1):
                            selections(dve, sel_made, s["ndone"], i.plus(1), c)

                    def body(i):
                        if kind == 0:
                            finish(i, 0)
                            if i.at_least(1):
                                result_stats(i.plus(-1))
                            next_stats(i)
                            if i.at_least(1):
                                scale_half(dve, "o", NT, i.plus(-1))
                            next_scales(i)
                            if has(i, 3):
                                bring_hT(i.plus(3))
                            finish(i, 1)
                            return
                        if kind == 2 and has(i, 2):
                            edge_messages(i.plus(2))
                        if i.at_least(1):
                            result_stats(i.plus(-1))
                        finish(i, 0)
                        if has(i, 3):
                            bring_hT(i.plus(3))
                        if kind == 1 and has(i, 2):
                            edge_messages(i.plus(2))
                        if i.at_least(1):
                            scale_half(dve, "o", NT, i.plus(-1))
                        finish(i, 1)
                    steps(body)(dve)
                    result_stats(number(LAST))
                    scale_half(dve, "o", NT, number(LAST))
                    dve.wait_ge(s["o_sh"], ITERS)

                def pe_program(pe):
                    def edge_transpose(e):
                        if e.at_least(1):
                            if kind == 0:
                                pe.wait_ge(s["emask"], e.value * R0)
                            else:
                                pe.wait_ge(s["eev"], e.value)
                        for k in range(J):
                            pe.wait_ge(s["eh"], e.value * J + (k + 1))
                            mm = pe.transpose(psum[:, 0, k * P:(k + 1) * P], hs[:, e.par, k, :], ident[:])
                        mm.then_inc(s["etr"], 1)

                    def edge_products(e):
                        if kind != 2 and e.at_least(1):
                            pe.wait_ge(s["msg"], e.value * J)
                        if kind == 0:
                            for r in range(R0):
                                pe.wait_ge(s["emask"], e.value * R0 + (r + 1))
                                for k in range(J):
                                    mm = pe.matmul(psum[:, 1, k * D:(k + 1) * D], masked[:, r, k * P:(k + 1) * P],
                                                   w_all[:, r * P:(r + 1) * P], start=r == k == 0,
                                                   stop=(r, k) == (R0 - 1, J - 1))
                            mm.then_inc(s["emm"], J)
                            return
                        pe.wait_ge(s["eev"], e.value + 1)
                        for k in range(J):
                            h = hT[:, k * P:(k + 1) * P]
                            if kind == 1:
                                for b in range(R1):
                                    mm = pe.matmul(psum[:, 1 + b, k * D:(k + 1) * D], h,
                                                   w_all[:, b * D:(b + 1) * D], start=True, stop=True)
                            else:
                                if k >= 2 or e.at_least(1):
                                    pe.wait_ge(s["mul"], e.value * 2 * J + 2 * (k - 1))
                                    pe.wait_ge(s["part"], e.value * J + (k - 1))
                                pe.matmul(psum[:, (1, 4)[k % 2], 0:C_W3], h, w_all[:, 0:C_W3],
                                          start=True, stop=True)
                                mm = pe.matmul(psum[:, 2 + k % 2, C_W3:C_END], h, w_all[:, C_W3:C_END],
                                               start=True, stop=True)
                            mm.then_inc(s["emm"], 1)

                    def node_transpose(i, c):
                        if i.at_least(1):
                            pe.wait_ge(s["nev"], i.value * 2 + (c - 1))
                        for k in range(J):
                            pe.wait_ge(s["nh"], i.value * NT + (c * J + k + 1))
                            mm = pe.transpose(psum[:, 3 + c, k * P:(k + 1) * P], nh[:, c * J + k, :], ident[:])
                        mm.then_inc(s["ntr"], 1)

                    def node_sums(i, c, windows):
                        ready(pe, s["msg"], sel_made, i, c)
                        if dense:
                            pe.wait_ge(s["nev"], i.value * 2 + (c + 1))
                        if i.at_least(1):
                            pe.wait_ge(s["res"], i.value * 2 + (c - 1))
                        sums(pe, i, c, windows, 5 + c, node_w if dense else None).then_inc(s["ndone"], 1)

                    if n_w:
                        pe.wait_ge(s["w"], 16 * n_w)
                    for e in (number(0), number(1)):
                        edge_transpose(e)
                        edge_products(e)
                    edge_transpose(number(2))
                    if dense:
                        node_transpose(number(0), 0)
                        node_transpose(number(0), 1)

                    def body(i):
                        windows = load_windows(i, mybir.EngineType.PE)
                        if kind == 2:
                            if has(i, 2):
                                edge_products(i.plus(2))
                            if has(i, 3):
                                edge_transpose(i.plus(3))
                            node_sums(i, 0, windows)
                            node_sums(i, 1, windows)
                            return
                        node_sums(i, 0, windows)
                        if has(i, 2):
                            edge_products(i.plus(2))
                        if has(i, 3):
                            edge_transpose(i.plus(3))
                        if dense and has(i, 1):
                            node_transpose(i.plus(1), 0)
                        node_sums(i, 1, windows)
                        if dense and has(i, 1):
                            node_transpose(i.plus(1), 1)
                    steps(body)(pe)

                with nc.Block() as block:
                    block.sync(sp_program)
                    block.gpsimd(pool_program)
                    block.scalar(act_program)
                    block.vector(dve_program)
                    block.tensor(pe_program)
                end_phase()

            def gated_layer(x_in):
                names = ["w", "bias", "sums", "ga0", "ga1", "nl0", "nl1", "st0", "st1", "index", "eh", "etr", "eev", "emm",
                         "dot", "att", "sig", "part", "msg", "sel0", "sel1", "nh", "ntr", "nev", "agg", "base", "atr",
                         "aT", "gate", "t1", "t2", "n", "d", "dz", "new", "res"]
                s = dict(zip(names, sems(*[f"s3_{n}" for n in names])))
                ga, nl, st, sel_made = ([s[f"{q}{a}"] for a in range(2)] for q in ("ga", "nl", "st", "sel"))
                weights = [
                    (w_all[:, 0:D], w_msg), (w_all[:, D:2 * D], b_msg.broadcast_to([P, D])),
                    (w_all[:, 2 * D:4 * D], w_att.broadcast_to([P, 2 * D])),
                    (w_all[:, 4 * D:4 * D + 1], b_att.broadcast_to([P, 1])),
                    (wi, w_ihT), (wh, w_hhT), (bvec[:, 0:3], b_ih), (bvec[:, 3:6], b_hh)]
                LAST_G = GROUPS - 1
                summed, change = masked[:, 0, :], masked[:, 1, :]
                hd_of = [masked[:, 2 + a, :].rearrange("p (j d) -> p j d", j=J) for a in range(2)]
                r_g, z_g, n_g, t_g = (masked[:, q, :] for q in range(4, 8))
                BANK_R, BANK_Z, BANK_NH, BANK_NI = (2, 4), (3, 5), 6, 7

                def group(i, c):
                    return i.value * 2 + c, c == 1 or i.at_least(1)

                def pool_program(pool):
                    def gather(e):
                        a = e.par
                        if e.at_least(2):
                            wait_apart(pool, s["eh"], e.value * 2 * J - 2 * J)
                        pool.tensor_copy(src_now[:, a, :], src_i[:, bass.ds(e.value * J, J)]).then_inc(s["index"], 1)
                        pool.tensor_copy(dst_now[:, a, :], dst_i[:, bass.ds(e.value * J, J)]).then_inc(s["index"], 1)
                        wait_apart(pool, s["index"], e.value * 2 + 2)
                        for k in range(J):
                            for rows, index in ((gxw, src_now), (gdw, dst_now)):
                                pool.indirect_dma_start(rows[:, a, k, :], None, x_in,
                                                        bass.IndirectOffsetOnAxis(index[:, a, k:k + 1], 0)
                                                        ).then_inc(ga[a], 16)

                    for e in range(4):
                        gather(number(e))

                    def body(i):
                        if has(i, 4):
                            gather(i.plus(4))
                    steps(body)(pool)

                def sp_program(sp):
                    for dst_ap, src_ap in weights:
                        sp.dma_start(dst_ap, src_ap).then_inc(s["w"], 16)

                    def load_nodes(i):
                        if i.at_least(2):
                            sp.wait_ge(s["nh"], i.value * NT - NT)
                        sp.dma_start(nx[:, i.par], x_in[bass.ds(i.value * (NT * P), NT * P), :]
                                     .rearrange("(j p) d -> p j d", p=P)).then_inc(nl[i.par], 16)

                    load_nodes(number(0))
                    load_nodes(number(1))

                    def body(i):
                        if has(i, 2):
                            load_nodes(i.plus(2))
                        sp.wait_ge(s["new"], i.value * 2 + 2)
                        sp.dma_start(newT[:, bass.ds(i.value * (NT * P), NT * P)],
                                     newT_now[:, i.par]).then_inc(st[i.par], 16)
                    steps(body)(sp)
                    sp.wait_ge(st[0], 16 * (LAST // 2 + 1))
                    sp.wait_ge(st[1], 16 * ((LAST + 1) // 2))

                def act_program(act):
                    def edge_relu(e):
                        a = e.par
                        act.wait_ge(ga[a], e.half * 32 * J + 32 * J)
                        if e.at_least(2):
                            act.wait_ge(s["etr"], e.value - 1)
                            act.wait_ge(s["dot"], e.value * 2 * J - 2 * J)
                        for out, rows in ((hs[:, a], gxw[:, a]), (hd_of[a], gdw[:, a])):
                            for k in range(J):
                                act.activation(out[:, k, :], rows[:, k, 0:D], ACT.Relu, bias=rows[:, k, D + 1:W],
                                               scale=rows[:, k, D:D + 1]).then_inc(s["eh"], 1)

                    def edge_sigmoid(e):
                        act.wait_ge(s["att"], e.value + 1)
                        act.activation(att_s[:, e.par, 2, :], att_s[:, e.par, 2, :], ACT.Sigmoid,
                                       bias=w_all[:, 4 * D:4 * D + 1]).then_inc(s["sig"], 1)

                    def edge_messages(e):
                        act.wait_ge(s["part"], e.value + 1)
                        act.wait_ge(s["sig"], e.value + 1)
                        for k in range(J):
                            act.activation(messages[:, bass.ds((e.value * J + k) * D, D)],
                                           prod[:, 0, k * D:(k + 1) * D], ACT.Copy,
                                           scale=att_s[:, e.par, 2, k:k + 1]).then_inc(s["msg"], 1)

                    def node_relu(i, c):
                        act.wait_ge(nl[i.par], i.half * 16 + 16)
                        if i.at_least(1):
                            act.wait_ge(s["ntr"], i.value * 2 + (c - 1))
                        for k in range(c * J, (c + 1) * J):
                            act.activation(nh[:, k, :], nx[:, i.par, k, 0:D], ACT.Relu,
                                           bias=nx[:, i.par, k, D + 1:W], scale=nx[:, i.par, k, D:D + 1]
                                           ).then_inc(s["nh"], 1)

                    def evacuate_h(i, c):
                        g, _ = group(i, c)
                        act.wait_ge(s["ntr"], g + 1)
                        if i.at_least(1):
                            act.wait_ge(s["d"], g - 1)
                        act.activation(nhT[:, c, :], psum[:, BANK_Z[c], :], ACT.Copy).then_inc(s["nev"], 1)

                    def evacuate_sums(i, c):
                        g, later = group(i, c)
                        act.wait_ge(s["agg"], g + 1)
                        if later:
                            act.wait_ge(s["atr"], g)
                        act.activation(summed, psum[:, 1, :], ACT.Copy).then_inc(s["base"], 1)

                    def gates(i, c):
                        g, later = group(i, c)
                        act.wait_ge(s["sums"], g + 1)
                        if later:
                            act.wait_ge(s["t1"], g)
                        act.activation(r_g, psum[:, BANK_R[c], :], ACT.Sigmoid, bias=bvec[:, 6:7]
                                       ).then_inc(s["gate"], 1)
                        if later:
                            act.wait_ge(s["dz"], g)
                        act.activation(z_g, psum[:, BANK_Z[c], :], ACT.Sigmoid, bias=bvec[:, 7:8]
                                       ).then_inc(s["gate"], 1)

                    def candidate(i, c):
                        g, later = group(i, c)
                        act.wait_ge(s["t2"], g + 1)
                        if later:
                            act.wait_ge(s["new"], g)
                        act.activation(n_g, t_g, ACT.Tanh, bias=bvec[:, 2:3]).then_inc(s["n"], 1)

                    act.wait_ge(s["w"], 16 * len(weights))
                    act.wait_ge(s["bias"], 1)
                    for e in (number(0), number(1)):
                        edge_relu(e)
                        edge_sigmoid(e)
                        edge_messages(e)
                    edge_relu(number(2))
                    for c in range(2):
                        node_relu(number(0), c)

                    def body(i):
                        if i.at_least(1):
                            gates(i.plus(-1), 1)
                        evacuate_h(i, 0)
                        evacuate_sums(i, 0)
                        if i.at_least(1):
                            candidate(i.plus(-1), 1)
                        if has(i, 3):
                            edge_relu(i.plus(3))
                        if has(i, 2):
                            edge_sigmoid(i.plus(2))
                        if has(i, 2):
                            edge_messages(i.plus(2))
                        gates(i, 0)
                        evacuate_h(i, 1)
                        evacuate_sums(i, 1)
                        candidate(i, 0)
                        if has(i, 1):
                            node_relu(i.plus(1), 0)
                            node_relu(i.plus(1), 1)
                    steps(body)(act)
                    gates(number(LAST), 1)
                    candidate(number(LAST), 1)

                def dve_program(dve):
                    def edge_dots(e):
                        a = e.par
                        dve.wait_ge(s["eh"], e.value * 2 * J + 2 * J)
                        if e.at_least(2):
                            dve.wait_ge(s["msg"], e.value * J - J)
                        for k in range(J):
                            for q, (h, w) in enumerate(((hs[:, a, k, :], w_all[:, 2 * D:3 * D]),
                                                        (hd_of[a][:, k, :], w_all[:, 3 * D:4 * D]))):
                                dve.tensor_tensor_reduce(prod[:, 1, (2 * k + q) * D:(2 * k + q + 1) * D], h, w,
                                                         1.0, 0.0, ALU.mult, ALU.add,
                                                         att_s[:, a, q, k:k + 1]).then_inc(s["dot"], 1)
                        dve.wait_ge(s["dot"], e.value * 2 * J + 2 * J)
                        dve.tensor_tensor(att_s[:, a, 2, :], att_s[:, a, 0, :], att_s[:, a, 1, :],
                                          ALU.add).then_inc(s["att"], 1)

                    def bring_hT(e):
                        dve.wait_ge(s["etr"], e.value + 1)
                        if e.at_least(1):
                            dve.wait_ge(s["emm"], e.value)
                        dve.tensor_copy(hT[:], psum[:, 0, :]).then_inc(s["eev"], 1)

                    def add_message_bias(e):
                        dve.wait_ge(s["emm"], e.value + 1)
                        if e.at_least(1):
                            dve.wait_ge(s["msg"], e.value * J)
                        dve.tensor_tensor(prod[:, 0, 0:GROUP].rearrange("p (j d) -> p j d", j=J),
                                          psum[:, 1, :].rearrange("p (j d) -> p j d", j=J),
                                          w_all[:, D:2 * D].rearrange("p (o d) -> p o d", o=1)
                                          .broadcast_to([P, J, D]), ALU.add).then_inc(s["part"], 1)

                    def bring_sums(i, c):
                        g, later = group(i, c)
                        dve.wait_ge(s["atr"], g + 1)
                        if later:
                            dve.wait_ge(s["sums"], g)
                        dve.tensor_copy(aT[:], psum[:, 0, :]).then_inc(s["aT"], 1)

                    def candidate_input(i, c):
                        g, later = group(i, c)
                        dve.wait_ge(s["gate"], g * 2 + 1)
                        if later:
                            dve.wait_ge(s["n"], g)
                        dve.scalar_tensor_tensor(out=t_g, in0=psum[:, BANK_NH, :], scalar=bvec[:, 5:6],
                                                 in1=r_g, op0=ALU.add, op1=ALU.mult).then_inc(s["t1"], 1)
                        dve.wait_ge(s["t1"], g + 1)
                        dve.tensor_tensor(t_g, psum[:, BANK_NI, :], t_g, ALU.add).then_inc(s["t2"], 1)

                    def update(i, c):
                        g, _ = group(i, c)
                        new = newT_now[:, i.par, c * GROUP:(c + 1) * GROUP]
                        dve.wait_ge(s["n"], g + 1)
                        dve.tensor_tensor(change, nhT[:, c, :], n_g, ALU.subtract).then_inc(s["d"], 1)
                        dve.wait_ge(s["d"], g + 1)
                        dve.wait_ge(s["gate"], g * 2 + 2)
                        dve.tensor_tensor(change, change, z_g, ALU.mult).then_inc(s["dz"], 1)
                        dve.wait_ge(s["dz"], g + 1)
                        if c == 0 and i.at_least(2):
                            dve.wait_ge(st[i.par], i.half * 16)
                        dve.tensor_tensor(new, change, n_g, ALU.add).then_inc(s["new"], 1)
                        dve.wait_ge(s["new"], g + 1)
                        last = isinstance(g, int) and g == LAST_G
                        dve.bn_stats(bn_st[:, bass.ds(g, 1), :].rearrange("p a c -> p (a c)"),
                                     new[:, 0:TAIL] if last else new).then_inc(s["res"], 1)

                    dve.wait_ge(s["w"], 16 * len(weights))
                    dve.tensor_tensor(bvec[:, 6:8], bvec[:, 0:2], bvec[:, 3:5], ALU.add).then_inc(s["bias"], 1)
                    for e in (number(0), number(1)):
                        edge_dots(e)
                        bring_hT(e)
                        add_message_bias(e)
                    for c in range(2):
                        selections(dve, sel_made, s["agg"], number(0), c)

                    def body(i):
                        if has(i, 2):
                            bring_hT(i.plus(2))
                        if i.at_least(1):
                            candidate_input(i.plus(-1), 1)
                        if has(i, 2):
                            edge_dots(i.plus(2))
                        bring_sums(i, 0)
                        if has(i, 2):
                            add_message_bias(i.plus(2))
                        if i.at_least(1):
                            update(i.plus(-1), 1)
                        candidate_input(i, 0)
                        if has(i, 1):
                            selections(dve, sel_made, s["agg"], i.plus(1), 0)
                        bring_sums(i, 1)
                        update(i, 0)
                        if has(i, 1):
                            selections(dve, sel_made, s["agg"], i.plus(1), 1)
                    steps(body)(dve)
                    candidate_input(number(LAST), 1)
                    update(number(LAST), 1)
                    dve.wait_ge(s["res"], GROUPS)

                def pe_program(pe):
                    def edge_transpose(e):
                        for k in range(J):
                            pe.wait_ge(s["eh"], e.value * 2 * J + (k + 1))
                            mm = pe.transpose(psum[:, 0, k * P:(k + 1) * P], hs[:, e.par, k, :], ident[:])
                        mm.then_inc(s["etr"], 1)

                    def edge_products(e):
                        pe.wait_ge(s["eev"], e.value + 1)
                        for k in range(J):
                            mm = pe.matmul(psum[:, 1, k * D:(k + 1) * D], hT[:, k * P:(k + 1) * P],
                                           w_all[:, 0:D], start=True, stop=True)
                        mm.then_inc(s["emm"], 1)

                    def half(i, c, windows):
                        g, later = group(i, c)
                        if i.at_least(1):
                            pe.wait_ge(s["gate"], g * 2 - 2)
                        for k in range(J):
                            pe.wait_ge(s["nh"], i.value * NT + (c * J + k + 1))
                            mm = pe.transpose(psum[:, BANK_Z[c], k * P:(k + 1) * P], nh[:, c * J + k, :], ident[:])
                        mm.then_inc(s["ntr"], 1)
                        ready(pe, s["msg"], sel_made, i, c)
                        pe.wait_ge(s["part"], i.value + (2 + c) if has(i, 1 + c) else ITERS)
                        sums(pe, i, c, windows, 1, None).then_inc(s["agg"], 1)
                        pe.wait_ge(s["nev"], g + 1)
                        h = nhT[:, c, :]
                        pe.matmul(psum[:, BANK_R[c], :], wh[:, 0:D], h, start=True, stop=False)
                        if later:
                            pe.wait_ge(s["t2"], g)
                        pe.matmul(psum[:, BANK_NH, :], wh[:, 2 * D:3 * D], h, start=True, stop=True)
                        if c == 0:
                            pe.wait_ge(s["eev"], i.value + 3 if has(i, 2) else ITERS)
                        pe.wait_ge(s["base"], g + 1)
                        for k in range(J):
                            mm = pe.transpose(psum[:, 0, k * P:(k + 1) * P], summed[:, k * P:(k + 1) * P], ident[:])
                        mm.then_inc(s["atr"], 1)
                        pe.matmul(psum[:, BANK_Z[c], :], wh[:, D:2 * D], h, start=True, stop=False)
                        if c == 0 and has(i, 2):
                            edge_products(i.plus(2))
                        pe.wait_ge(s["aT"], g + 1)
                        pe.matmul(psum[:, BANK_R[c], :], wi[:, 0:D], aT[:], start=False, stop=True)
                        pe.matmul(psum[:, BANK_Z[c], :], wi[:, D:2 * D], aT[:], start=False, stop=True)
                        pe.matmul(psum[:, BANK_NI, :], wi[:, 2 * D:3 * D], aT[:], start=True, stop=True
                                  ).then_inc(s["sums"], 1)

                    pe.wait_ge(s["w"], 16 * len(weights))
                    for e in (number(0), number(1)):
                        if e.value:
                            pe.wait_ge(s["part"], 1)
                        edge_transpose(e)
                        edge_products(e)
                    edge_transpose(number(2))

                    def body(i):
                        windows = load_windows(i, mybir.EngineType.PE)
                        half(i, 0, windows)
                        half(i, 1, windows)
                        if has(i, 3):
                            edge_transpose(i.plus(3))
                    steps(body)(pe)

                with nc.Block() as block:
                    block.sync(sp_program)
                    block.gpsimd(pool_program)
                    block.scalar(act_program)
                    block.vector(dve_program)
                    block.tensor(pe_program)
                end_phase()


            fused("s0", 0, x, x1, [(w_all[:, 0:R0 * P].rearrange("p (r o) -> p r o", r=R0),
                                    w_rel.rearrange("r i o -> i r o"))], root)

            fused("s1", 1, x1, x2, [(w_all[:, 0:R1 * D].rearrange("p (b o) -> p b o", b=R1),
                                     bases.rearrange("b i o -> i b o"))], self_w)

            ld, step, acc = sems("s2_ld", "s2_step", "s2_acc")
            pairs = spherical_pairs()
            with nc.Block() as block:
                spread = prod[:, 0, 0:5 * 32].rearrange("p (k w) -> p k w", k=5)
                sph_s = prod[:, 1, 0:R2 * 4].rearrange("p (m c) -> p m c", m=R2)
                cols_s = prod[:, 1, 64:71]
                at3 = coef[:].rearrange("p (t m) -> p t m", m=R2)
                mix3 = mix[:].rearrange("p (t c) -> p t c", c=9)

                @block.sync
                def _(sp):
                    sp.dma_start(prod[:, 1, 0:R2 * 4], sph.rearrange("p m c -> p (m c)")).then_inc(ld, 16)
                    sp.dma_start(cols_s, sph_cols).then_inc(ld, 16)
                    sp.dma_start(coef[:], attr).then_inc(ld, 16)
                    sp.wait_ge(step, 1)
                    for k, w in enumerate((w0, w1)):
                        sp.dma_start(spread[0:32, k, :], w.rearrange("u a w -> u (a w)")).then_inc(ld, 16)
                    for k, w in enumerate((w2, w3, w4)):
                        for i in range(3):
                            sp.dma_start(spread[32 + i:P:3, 2 + k, :],
                                         w.rearrange("u a w -> u (a w)")).then_inc(ld, 16)
                    sp.wait_ge(ld, 16 * 14)

                @block.vector
                def _(dve):
                    dve.memset(prod[:, 0, 0:5 * 32], 0.0).then_inc(step, 1)
                    dve.wait_ge(ld, 16 * 14)
                    dve.tensor_scalar(w_all[:, 0:32], spread[:, 0, :], sph_s[:, 0, 0:1], None, ALU.mult)
                    for k in range(3):
                        dve.tensor_scalar(w_all[:, 32 + k:D:3], spread[:, 2, :], sph_s[:, 0, 1 + k:2 + k],
                                          None, ALU.mult)
                    dve.tensor_scalar(w_all[:, C_W1:C_W3], spread[:, 1, :], cols_s[:, 0:1], None, ALU.mult)
                    for i in range(3):
                        dve.tensor_scalar(w_all[:, C_W3 + i:C_W4:3], spread[:, 3, :], cols_s[:, 1 + i:2 + i],
                                          None, ALU.mult)
                        dve.tensor_scalar(w_all[:, C_W4 + i:C_END:3], spread[:, 4, :], cols_s[:, 4 + i:5 + i],
                                          None, ALU.mult)
                    n = 0
                    for (i, k), terms in pairs.items():
                        out = mix3[:, :, 3 * k + i]
                        for q, (j, f) in enumerate(terms):
                            y = at3[:, :, 4 + j]
                            if q == 0:
                                dve.tensor_scalar(out, y, f, None, ALU.mult).then_inc(acc, 1)
                            else:
                                dve.wait_ge(acc, n)
                                dve.scalar_tensor_tensor(out=out, in0=y, scalar=f, in1=out, op0=ALU.mult,
                                                         op1=ALU.add).then_inc(acc, 1)
                            n += 1
                    dve.drain()
            end_phase()
            fused("s2", 2, x2, x3, [])

            gated_layer(x3)
            last_phase("s4", x3)

        def general(own):
            before = sb("before", P, P, keep=own)
            onehot = sb("onehot", P, TILES, R0, keep=own)
            same = sb("same", P, J, P, keep=own)

            x1, x2, x3 = table("x1", ROWS, D), table("x2", ROWS, D), table("x3", ROWS, D)
            agg, counts = table("agg", ROWS, D), table("counts", ROWS, R0)
            ld, const, step, rep = sems("gen_ld", "gen_const", "gen_step", "gen_rep")
            with nc.Block() as block:
                @block.sync
                def _(sp):
                    sp.dma_start(dst_row[:], dst_flat.broadcast_to([P, EDGES])).then_inc(ld, 16)
                    sp.dma_start(coef[:, 0:TILES].bitcast(I32), type8).then_inc(ld, 16)
                    sp.dma_start(w_all[:, 0:R0 * P].rearrange("p (r o) -> p r o", r=R0),
                                 w_rel.rearrange("r i o -> i r o")).then_inc(ld, 16)
                    sp.wait_ge(ld, 48)

                @block.gpsimd
                def _(pool):
                    pool.memset(before[:], 1.0).then_inc(const, 1)
                    pool.iota(dump_f[:], [[0, 1]], base=DUMP, channel_multiplier=1,
                              allow_small_or_imprecise_dtypes=True).then_inc(const, 1)
                    pool.wait_ge(const, 2)
                    pool.affine_select(out=before[:], in_=before[:], compare_op=ALU.is_gt, fill=0.0,
                                       base=0, pattern=[[-1, P]], channel_multiplier=1).then_inc(const, 1)

                @block.vector
                def _(dve):
                    dve.memset(onehot[:], 0.0).then_inc(step, 1)
                    dve.wait_ge(ld, 48)
                    dve.wait_ge(const, 3)
                    dve.wait_ge(step, 1)
                    kind = coef[:, 0:TILES].bitcast(I32)
                    for r in range(R0):
                        dve.tensor_scalar(onehot[:, :, r], kind, float(r), None, ALU.is_equal)
                    with dve.Fori(0, ITERS) as it:
                        for k in range(J):
                            dve.scalar_tensor_tensor(
                                out=same[:, k, :], in0=dst_row[:, bass.ds(it * GROUP + k * P, P)],
                                scalar=dst_f[:, bass.ds(it * J + k, 1)], in1=before[:],
                                op0=ALU.is_equal, op1=ALU.mult).then_inc(rep, 1)
                        dve.wait_ge(rep, it * J + J)
                        dve.tensor_reduce(repeat[:, bass.ds(it * J, J)], same[:], AX_X,
                                          ALU.max).then_inc(step, 1)
                        dve.wait_ge(step, it + 2)
                    dve.tensor_scalar(std[:, 0:1], dump_f[:], -1.0, None, ALU.mult).then_inc(step, 1)
                    dve.wait_ge(step, ITERS + 2)
                    dve.tensor_scalar(coef[:, 0:TILES], dst_f[:], std[:, 0:1], -1.0, ALU.add,
                                      ALU.mult).then_inc(step, 1)
                    dve.wait_ge(step, ITERS + 3)
                    dve.tensor_tensor(coef[:, 0:TILES], coef[:, 0:TILES], repeat[:], ALU.mult).then_inc(step, 1)
                    dve.wait_ge(step, ITERS + 4)
                    dve.tensor_tensor(scat_i[:], coef[:, 0:TILES], dst_f[:], ALU.add).then_inc(step, 1)
                    dve.wait_ge(step, ITERS + 5)
            end_phase()

            zs, zd = sems("zero_set", "zero_dma")
            with nc.Block() as block:
                @block.vector
                def _(dve):
                    dve.memset(gx[:], 0.0).then_inc(zs, 1)

                @block.sync
                def _(sp):
                    sp.wait_ge(zs, 1)
                    flat = gx[:].rearrange("p a j d -> p (a j d)")
                    n = 0
                    width = ROWS * R0 // P
                    for at in range(0, width, 1024):
                        w = min(1024, width - at)
                        sp.dma_start(counts.rearrange("(p a) r -> p (a r)", p=P)[:, at:at + w],
                                     flat[:, 0:w]).then_inc(zd, 16)
                        n += 1
                    with sp.Fori(0, GROUPS // 2) as it:
                        sp.dma_start(agg[bass.ds(it * 2 * GROUP, 2 * GROUP), :]
                                     .rearrange("(j p) d -> p j d", p=P),
                                     gx[:].rearrange("p a j d -> p (a j) d")).then_inc(zd, 16)
                    sp.wait_ge(zd, 16 * (n + GROUPS // 2))
            end_phase()

            eq_s, pe_s, ev_s, sc_s, ix_s, free_s = sems("cnt_eq", "cnt_pe", "cnt_ev", "cnt_scat", "cnt_index",
                                                       "cnt_free")
            with nc.Block() as block:
                @block.vector
                def _(dve):
                    with dve.Fori(0, ITERS) as it:
                        for k in range(J):
                            dve.tensor_scalar(same[:, k, :], dst_row[:, bass.ds(it * GROUP + k * P, P)],
                                              dst_f[:, bass.ds(it * J + k, 1)], None,
                                              ALU.is_equal).then_inc(eq_s, 1)
                        dve.wait_ge(pe_s, it * J + J)
                        dve.wait_ge(free_s, it + 1)
                        dve.tensor_copy(comb[:, :, 0:R0],
                                        psum[:, 0, 0:J * R0].rearrange("p (j r) -> p j r", j=J)).then_inc(ev_s, 1)

                @block.tensor
                def _(pe):
                    with pe.Fori(0, ITERS) as it:
                        for k in range(J):
                            pe.wait_ge(eq_s, it * J + (k + 1))
                            pe.matmul(psum[:, 0, k * R0:(k + 1) * R0], same[:, k, :],
                                      onehot[:, bass.ds(it * J + k, 1), :].rearrange("p a r -> p (a r)"),
                                      start=True, stop=True).then_inc(pe_s, 1)

                @block.gpsimd
                def _(pool):
                    pool.sem_inc(free_s, 1)
                    with pool.Fori(0, ITERS) as it:
                        pool.tensor_copy(scat_now[:], scat_i[:, bass.ds(it * J, J)]).then_inc(ix_s, 1)
                        wait_apart(pool, ix_s, it + 1)
                        wait_apart(pool, ev_s, it + 1)
                        for k in range(J):
                            pool.indirect_dma_start(
                                counts, bass.IndirectOffsetOnAxis(scat_now[:, k:k + 1], 0),
                                comb[:, k, 0:R0], None, compute_op=ALU.add).then_inc(sc_s, 16)
                            wait_apart(pool, sc_s, it * (16 * J) + 16 * (k + 1))
                        pool.sem_inc(free_s, 1)
            end_phase()

            cg0, cg1, ci, cm, cc = sems("cof_ga0", "cof_ga1", "cof_index", "cof_mul", "cof_copy")
            with nc.Block() as block:
                cnt = coef[:, 0:TILES * R0]
                @block.gpsimd
                def _(pool):
                    pool.sem_inc(cc, 2)

                    def body(it, a):
                        pool.wait_ge(cc, it + 1)
                        pool.tensor_copy(dst_now[:, a, :], dst_i[:, bass.ds(it * J, J)]).then_inc(ci, 1)
                        wait_apart(pool, ci, it + 1)
                        for k in range(J):
                            pool.indirect_dma_start(gx[:, a, k, 0:R0], None, counts,
                                                    bass.IndirectOffsetOnAxis(dst_now[:, a, k:k + 1], 0)
                                                    ).then_inc((cg0, cg1)[a], 16)
                    with pool.Fori(0, ITERS // 2) as pair:
                        for a in range(2):
                            body(pair * 2 + a, a)
                    body(ITERS - 1, 0)

                @block.vector
                def _(dve):
                    def body(it, pair, a):
                        dve.wait_ge((cg0, cg1)[a], pair * (16 * J) + 16 * J)
                        dve.tensor_copy(cnt[:, bass.ds(it * (J * R0), J * R0)].rearrange("p (j r) -> p j r", j=J),
                                        gx[:, a, :, 0:R0]).then_inc(cc, 1)
                    with dve.Fori(0, ITERS // 2) as pair:
                        for a in range(2):
                            body(pair * 2 + a, pair, a)
                    body(ITERS - 1, ITERS // 2, 0)
                    dve.wait_ge(cc, ITERS + 2)
                    oh = onehot[:].rearrange("p t r -> p (t r)")
                    dve.tensor_scalar(cnt, cnt, 1.0, None, ALU.max).then_inc(cm, 1)
                    dve.wait_ge(cm, 1)
                    dve.reciprocal(cnt, cnt).then_inc(cm, 1)
                    dve.wait_ge(cm, 2)
                    dve.tensor_tensor(cnt, cnt, oh, ALU.mult).then_inc(cm, 1)
                    dve.wait_ge(cm, 3)
            end_phase()

            def norm_dve(dve, s, rows, n, base, it, sq_waits):
                for k in range(n):
                    dve.bn_stats(stats[:, k, :], rows(k)).then_inc(s["stat"], 1)
                wait_apart(dve, s["stat"], it * n + n)
                for k in range(n):
                    ins = dve.bn_aggr(mv[:, k, :], stats[:, k, :])
                    ins.then_inc(s["mv"], 1)
                dve.wait_ge(s["mv"], it * n + n)
                dve.tensor_scalar(std[:, 0:n], mv[:, 0:n, 1], EPS, None, ALU.add).then_inc(s["var"], 1)
                dve.wait_ge(s["std"], it + 1)
                dve.reciprocal(rstd[:, 0:n], std[:, 0:n]).then_inc(s["rstd"], 1)
                dve.wait_ge(s["rstd"], it + 1)
                dve.scalar_tensor_tensor(out=shift[:, 0:n], in0=mv[:, 0:n, 0], scalar=-1.0,
                                         in1=rstd[:, 0:n], op0=ALU.mult, op1=ALU.mult).then_inc(s["shift"], 1)

            def norm_act(act, s, n, it):
                act.wait_ge(s["var"], it + 1)
                act.activation(std[:, 0:n], std[:, 0:n], ACT.Sqrt).then_inc(s["std"], 1)
                act.wait_ge(s["shift"], it + 1)

            def norm_sems(name):
                names = ["stat", "mv", "var", "std", "rstd", "shift"]
                return dict(zip(names, sems(*[f"{name}_{n}" for n in names])))

            def dense_phase(name, x_in, x_out, w_dram, with_bias):
                s = norm_sems(name)
                w_ld, ld0, ld1, st0, st1, h_s, tr_s, ev_s, mm_s, res_s, xb_s = sems(
                    *[f"{name}_{n}" for n in ("w", "ld0", "ld1", "st0", "st1", "h", "tr", "ev", "mm",
                                              "res", "xb")])
                loaded, stored = (ld0, ld1), (st0, st1)
                w = aT[:, 0:D]
                res = gd
                with nc.Block() as block:
                    @block.sync
                    def _(sp):
                        sp.dma_start(w, w_dram).then_inc(w_ld, 16)
                        sp.sem_inc(res_s, 2)
                        with sp.Fori(0, GROUPS // 2) as it:
                            for a in range(2):
                                sp.wait_ge(res_s, it * 2 + (a + 1))
                                sp.dma_start(gx[:, a], x_in[bass.ds((it * 2 + a) * GROUP, GROUP), :]
                                             .rearrange("(j p) d -> p j d", p=P)).then_inc(loaded[a], 16)

                    @block.vector
                    def _(dve):
                        def body(it):
                            for a in range(2):
                                g = it * 2 + a
                                dve.wait_ge(loaded[a], it * 16 + 16)
                                norm_dve(dve, s, lambda k: gx[:, a, k, :], J, 0, g, None)
                                dve.wait_ge(tr_s, g * J + J)
                                dve.tensor_copy(hT[:], psum[:, 0, :]).then_inc(ev_s, 1)
                                if with_bias:
                                    for k in range(J):
                                        dve.tensor_tensor(prod[:, a, k * D:(k + 1) * D], gx[:, a, k, :],
                                                          b_row[:], ALU.add).then_inc(xb_s, 1)
                                    dve.wait_ge(xb_s, g * J + J)
                                    base = prod[:, a, 0:GROUP]
                                else:
                                    base = gx[:, a].rearrange("p j d -> p (j d)")
                                dve.wait_ge(mm_s, g * J + J)
                                if not first(it):
                                    dve.wait_ge(stored[a], it * 16)
                                dve.tensor_tensor(res[:, a].rearrange("p j d -> p (j d)"), psum[:, 1, :],
                                                  base, ALU.add).then_inc(res_s, 1)
                        body(0)
                        with dve.Fori(1, GROUPS // 2) as it:
                            body(it)

                    @block.scalar
                    def _(act):
                        with act.Fori(0, GROUPS // 2) as it:
                            for a in range(2):
                                g = it * 2 + a
                                norm_act(act, s, J, g)
                                for k in range(J):
                                    act.activation(hs[:, a, k, :], gx[:, a, k, :], ACT.Relu,
                                                   bias=shift[:, k:k + 1], scale=rstd[:, k:k + 1]).then_inc(h_s, 1)
                                act.wait_ge(res_s, g + 3)
                                act.dma_start(x_out[bass.ds(g * GROUP, GROUP), :]
                                              .rearrange("(j p) d -> p j d", p=P), res[:, a]).then_inc(stored[a], 16)
                        for q in stored:
                            act.wait_ge(q, 16 * (GROUPS // 2))

                    @block.tensor
                    def _(pe):
                        pe.wait_ge(w_ld, 16)
                        with pe.Fori(0, GROUPS // 2) as it:
                            for a in range(2):
                                g = it * 2 + a
                                for k in range(J):
                                    pe.wait_ge(h_s, g * J + (k + 1))
                                    pe.transpose(psum[:, 0, k * P:(k + 1) * P], hs[:, a, k, :],
                                                 ident[:]).then_inc(tr_s, 1)
                                pe.wait_ge(ev_s, g + 1)
                                for k in range(J):
                                    pe.matmul(psum[:, 1, k * D:(k + 1) * D], hT[:, k * P:(k + 1) * P], w,
                                              start=True, stop=True).then_inc(mm_s, 1)
                end_phase()

            def edge_phase(name, x_in, x_out, products, gate=False):
                s = norm_sems(name)
                (ga0, ga1, h_s, tr_s, ev_s, mm_s, pr_s, msg_s, eq_s, sum_s, cb_s, sc_s, dot_s, gate_s,
                 sig_s, ix_s, sx_s, free_s) = sems(
                    *[f"{name}_{n}" for n in ("ga0", "ga1", "h", "tr", "ev", "mm", "prod", "msg", "eq",
                                              "sum", "comb", "scat", "dot", "gate", "sig", "index", "target", "free")])
                gathered = (ga0, ga1)
                n = 2 * J if gate else J
                per = (2 * J if gate else J)
                width = products * D
                banks = -(-width // PB)
                with nc.Block() as block:
                    @block.gpsimd
                    def _(pool):
                        def indices(it, a, count):
                            pool.tensor_copy(src_now[:, a, :], src_i[:, bass.ds(it * J, J)]).then_inc(ix_s, 1)
                            if gate:
                                pool.tensor_copy(dst_now[:, a, :], dst_i[:, bass.ds(it * J, J)]).then_inc(ix_s, 1)
                            wait_apart(pool, ix_s, count)

                        def gather(a, k):
                            pool.indirect_dma_start(gx[:, a, k, :], None, x_in,
                                                    bass.IndirectOffsetOnAxis(src_now[:, a, k:k + 1], 0)
                                                    ).then_inc(gathered[a], 16)
                            if gate:
                                pool.indirect_dma_start(gd[:, a, k, :], None, x_in,
                                                        bass.IndirectOffsetOnAxis(dst_now[:, a, k:k + 1], 0)
                                                        ).then_inc(gathered[a], 16)

                        lists = 2 if gate else 1

                        def body(it, a, more):
                            pool.tensor_copy(scat_now[:], scat_i[:, bass.ds(it * J, J)]).then_inc(sx_s, 1)
                            wait_apart(pool, sx_s, it + 1)
                            wait_apart(pool, cb_s, it + 1)
                            if more:
                                indices(it + 2, a, (it + 3) * lists)
                            for k in range(J):
                                pool.indirect_dma_start(x_out, bass.IndirectOffsetOnAxis(scat_now[:, k:k + 1], 0),
                                                        comb[:, k, :], None, compute_op=ALU.add).then_inc(sc_s, 16)
                                if more:
                                    gather(a, k)
                                wait_apart(pool, sc_s, it * (16 * J) + 16 * (k + 1))
                            pool.sem_inc(free_s, 1)

                        pool.sem_inc(free_s, 1)
                        for a in range(2):
                            indices(a, a, (a + 1) * lists)
                            for k in range(J):
                                gather(a, k)
                        with pool.Fori(0, (ITERS - 3) // 2) as pair:
                            for a in range(2):
                                body(pair * 2 + a, a, True)
                        for it in range(ITERS - 3, ITERS):
                            body(it, it % 2, it + 2 < ITERS)

                    def groups(engine, body):
                        with engine.Fori(0, ITERS // 2) as pair:
                            for a in range(2):
                                body(pair * 2 + a, pair, a)
                        body(ITERS - 1, ITERS // 2, 0)

                    @block.vector
                    def _(dve):
                        def body(it, pair, a):
                            dve.wait_ge(gathered[a], pair * (16 * per) + 16 * per)
                            norm_dve(dve, s, lambda k: gx[:, a, k, :] if k < J else gd[:, a, k - J, :],
                                     n, 0, it, None)
                            for k in range(J):
                                dve.tensor_scalar(same[:, k, :], dst_row[:, bass.ds(it * GROUP + k * P, P)],
                                                  dst_f[:, bass.ds(it * J + k, 1)], None,
                                                  ALU.is_equal).then_inc(eq_s, 1)
                            if gate:
                                dve.wait_ge(h_s, it * n + n)
                                for k in range(J):
                                    for e, (h, w) in enumerate(((hs[:, a, k, :], w_all[:, 2 * D:3 * D]),
                                                                (hd[:, k, :], w_all[:, 3 * D:4 * D]))):
                                        dve.tensor_tensor_reduce(prod[:, e, k * D:(k + 1) * D], h, w, 1.0, 0.0,
                                                                 ALU.mult, ALU.add, att[:, e, k:k + 1]).then_inc(dot_s, 1)
                                dve.wait_ge(dot_s, it * 2 * J + 2 * J)
                                dve.tensor_tensor(att[:, 2, :], att[:, 0, :], att[:, 1, :], ALU.add).then_inc(gate_s, 1)
                            dve.wait_ge(tr_s, it * J + J)
                            dve.tensor_copy(hT[:], psum[:, 0, :]).then_inc(ev_s, 1)
                            if gate:
                                dve.wait_ge(sig_s, it + 1)
                            for k in range(J):
                                t = it * J + k
                                dve.wait_ge(mm_s, t + 1)
                                b = 1 + 3 * (k % 2)
                                if gate:
                                    dve.tensor_tensor(prod[:, k % 2, 0:D], psum[:, b, 0:D], w_all[:, D:2 * D],
                                                      ALU.add).then_inc(pr_s, 1)
                                    dve.wait_ge(pr_s, t + 1)
                                    dve.tensor_scalar(msg[:, k, :], prod[:, k % 2, 0:D], att[:, 2, k:k + 1],
                                                      None, ALU.mult).then_inc(msg_s, 1)
                                    continue
                                ps = psum[:, b:b + 3, :].rearrange("p b c -> p (b c)")[:, 0:width]
                                cf = coef[:, bass.ds(t * products, products)]
                                dve.tensor_tensor(
                                    prod[:, k % 2, 0:width].rearrange("p (r o) -> p r o", r=products),
                                    ps.rearrange("p (r o) -> p r o", r=products),
                                    cf.rearrange("p (r o) -> p r o", o=1).broadcast_to([P, products, D]),
                                    ALU.mult).then_inc(pr_s, 1)
                                dve.wait_ge(pr_s, t + 1)
                                dve.tensor_reduce(msg[:, k, :],
                                                  prod[:, k % 2, 0:width].rearrange("p (r o) -> p o r", r=products),
                                                  AX_X, ALU.add).then_inc(msg_s, 1)
                            dve.wait_ge(sum_s, it * J + J)
                            dve.wait_ge(free_s, it + 1)
                            dve.tensor_copy(comb[:].rearrange("p j d -> p (j d)"), psum[:, 7, :]).then_inc(cb_s, 1)
                        groups(dve, body)

                    @block.scalar
                    def _(act):
                        def body(it, pair, a):
                            norm_act(act, s, n, it)
                            for k in range(n):
                                o = hs[:, a, k, :] if k < J else hd[:, k - J, :]
                                i = gx[:, a, k, :] if k < J else gd[:, a, k - J, :]
                                act.activation(o, i, ACT.Relu, bias=shift[:, k:k + 1],
                                               scale=rstd[:, k:k + 1]).then_inc(h_s, 1)
                            if gate:
                                act.wait_ge(gate_s, it + 1)
                                act.activation(att[:, 2, :], att[:, 2, :], ACT.Sigmoid,
                                               bias=w_all[:, 4 * D:4 * D + 1]).then_inc(sig_s, 1)
                        groups(act, body)

                    @block.tensor
                    def _(pe):
                        def body(it, pair, a):
                            for k in range(J):
                                pe.wait_ge(h_s, it * n + (k + 1))
                                pe.transpose(psum[:, 0, k * P:(k + 1) * P], hs[:, a, k, :],
                                             ident[:]).then_inc(tr_s, 1)
                            pe.wait_ge(ev_s, it + 1)

                            def combine(k):
                                pe.wait_ge(msg_s, it * J + (k + 1))
                                if k == 0:
                                    pe.wait_ge(eq_s, it * J + J)
                                pe.matmul(psum[:, 7, k * D:(k + 1) * D], same[:, k, :], msg[:, k, :],
                                          start=True, stop=True).then_inc(sum_s, 1)

                            for k in range(J):
                                if k >= 2:
                                    combine(k - 2)
                                b = 1 + 3 * (k % 2)
                                for q in range(banks):
                                    lo, hi = q * PB, min((q + 1) * PB, width)
                                    mm = pe.matmul(psum[:, b + q, 0:hi - lo], hT[:, k * P:(k + 1) * P],
                                                   w_all[:, lo:hi], start=True, stop=True)
                                mm.then_inc(mm_s, 1)
                            combine(J - 2)
                            combine(J - 1)
                        groups(pe, body)
                end_phase()

            dense_phase("d0", x, x1, root, True)
            edge_phase("e0", x, x1, R0)

            basis_coefficients("g1c", onehot)
            dense_phase("d1", x1, x2, self_w, False)
            edge_phase("e1", x1, x2, R1)

            ld2, c2, cp2 = sems("l2_ld", "l2_step", "l2_copy")
            with nc.Block() as block:
                spread = prod[:, 0, 0:5 * 32].rearrange("p (k w) -> p k w", k=5)
                sph_s = prod[:, 1, 0:R2 * 4].rearrange("p (m c) -> p m c", m=R2)
                wm = w_all[:].rearrange("p (m o) -> p m o", m=R2)

                @block.sync
                def _(sp):
                    sp.dma_start(prod[:, 1, 0:R2 * 4], sph.rearrange("p m c -> p (m c)")).then_inc(ld2, 16)
                    sp.dma_start(coef[:], attr).then_inc(ld2, 16)
                    sp.wait_ge(c2, 1)
                    for k, w in enumerate((w0, w1)):
                        sp.dma_start(spread[0:32, k, :], w.rearrange("u a w -> u (a w)")).then_inc(ld2, 16)
                    for k, w in enumerate((w2, w3, w4)):
                        for i in range(3):
                            sp.dma_start(spread[32 + i:P:3, 2 + k, :],
                                         w.rearrange("u a w -> u (a w)")).then_inc(ld2, 16)
                    with sp.Fori(0, GROUPS // 2) as it:
                        sp.dma_start(x3[bass.ds(it * 2 * GROUP, 2 * GROUP), :],
                                     x2[bass.ds(it * 2 * GROUP, 2 * GROUP), :]).then_inc(cp2, 16)
                    sp.wait_ge(cp2, 16 * (GROUPS // 2))

                @block.vector
                def _(dve):
                    dve.memset(prod[:, 0, 0:5 * 32], 0.0).then_inc(c2, 1)
                    dve.wait_ge(ld2, 16 * 13)
                    first = spread[:, 0, :]
                    for m in range(R2):
                        s0 = (0, 3)[m in (1, 2, 3)]
                        s1 = 2 if m == 0 else (1 if m < 4 else 4)
                        dve.tensor_scalar(wm[:, m, 0:32], spread[:, s0, :], sph_s[:, m, 0:1], None, ALU.mult)
                        for k in range(3):
                            dve.tensor_scalar(wm[:, m, 32 + k:D:3], spread[:, s1, :], sph_s[:, m, 1 + k:2 + k],
                                              None, ALU.mult)
                    dve.drain()
            end_phase()

            edge_phase("e2", x2, x3, R2)

            (ld3,) = sems("l3_ld")
            with nc.Block() as block:
                @block.sync
                def _(sp):
                    sp.dma_start(w_all[:, 0:D], w_msg).then_inc(ld3, 16)
                    sp.dma_start(w_all[:, D:2 * D], b_msg.broadcast_to([P, D])).then_inc(ld3, 16)
                    sp.dma_start(w_all[:, 2 * D:4 * D], w_att.broadcast_to([P, 2 * D])).then_inc(ld3, 16)
                    sp.dma_start(w_all[:, 4 * D:4 * D + 1], b_att.broadcast_to([P, 1])).then_inc(ld3, 16)
                    sp.wait_ge(ld3, 64)
            end_phase()
            edge_phase("e3", x3, agg, 1, gate=True)

            s = norm_sems("u")
            (w_ld, b_st, ld0, ld1_, st0, st1, h_s, tr_s, ev_s, mm_s, r_s, z_s, t1_s, t2_s, n_s, d_s, e_s, new_s,
             bn_s) = sems(*[f"u_{n}" for n in ("w", "b", "ld0", "ld1", "st0", "st1", "h", "tr", "ev", "mm", "r", "z",
                                               "t1", "t2", "n", "d", "e", "new", "bn")])
            loaded, stored = (ld0, ld1_), (st0, st1)
            rg, zg, ng, tg = (prod[:, 0, 0:GROUP], prod[:, 0, GROUP:2 * GROUP],
                              prod[:, 1, 0:GROUP], prod[:, 1, GROUP:2 * GROUP])
            new = [msg[:].rearrange("p j d -> p (j d)"), same[:].rearrange("p j d -> p (j d)")]
            with nc.Block() as block:
                @block.sync
                def _(sp):
                    sp.dma_start(wi, w_ihT).then_inc(w_ld, 16)
                    sp.dma_start(wh, w_hhT).then_inc(w_ld, 16)
                    sp.dma_start(bvec[:, 0:3], b_ih).then_inc(w_ld, 16)
                    sp.dma_start(bvec[:, 3:6], b_hh).then_inc(w_ld, 16)
                    sp.sem_inc(tr_s, 2)
                    with sp.Fori(0, GROUPS // 2) as it:
                        for a in range(2):
                            g = it * 2 + a
                            sp.wait_ge(tr_s, g + 1)
                            for buf, tab in ((gx, x3), (gd, agg)):
                                sp.dma_start(buf[:, a], tab[bass.ds(g * GROUP, GROUP), :]
                                             .rearrange("(j p) d -> p j d", p=P)).then_inc(loaded[a], 16)

                @block.scalar
                def _(act):
                    act.wait_ge(b_st, 1)
                    with act.Fori(0, GROUPS // 2) as it:
                        for a in range(2):
                            g = it * 2 + a
                            norm_act(act, s, J, g)
                            for k in range(J):
                                act.activation(hs[:, a, k, :], gx[:, a, k, :], ACT.Relu,
                                               bias=shift[:, k:k + 1], scale=rstd[:, k:k + 1]).then_inc(h_s, 1)
                            act.wait_ge(mm_s, g + 1)
                            act.activation(rg, psum[:, 2, :], ACT.Sigmoid, bias=bvec[:, 6:7]).then_inc(r_s, 1)
                            act.activation(zg, psum[:, 3, :], ACT.Sigmoid, bias=bvec[:, 7:8]).then_inc(z_s, 1)
                            act.wait_ge(t2_s, g + 1)
                            act.activation(ng, tg, ACT.Tanh, bias=bvec[:, 2:3]).then_inc(n_s, 1)
                            act.wait_ge(new_s, g + 1)
                            act.dma_start(newT[:, bass.ds(g * GROUP, GROUP)], new[a]).then_inc(stored[a], 16)
                    for q in stored:
                        act.wait_ge(q, 16 * (GROUPS // 2))

                @block.vector
                def _(dve):
                    dve.wait_ge(w_ld, 64)
                    dve.tensor_tensor(bvec[:, 6:8], bvec[:, 0:2], bvec[:, 3:5], ALU.add).then_inc(b_st, 1)
                    def body(it):
                        for a in range(2):
                            g = it * 2 + a
                            dve.wait_ge(loaded[a], it * 32 + 32)
                            norm_dve(dve, s, lambda k: gx[:, a, k, :], J, 0, g, None)
                            dve.wait_ge(tr_s, g + 3)
                            dve.tensor_copy(hT[:], psum[:, 0, :]).then_inc(ev_s, 1)
                            dve.tensor_copy(aT[:], psum[:, 1, :]).then_inc(ev_s, 1)
                            dve.wait_ge(r_s, g + 1)
                            dve.scalar_tensor_tensor(out=tg, in0=psum[:, 5, :], scalar=bvec[:, 5:6], in1=rg,
                                                     op0=ALU.add, op1=ALU.mult).then_inc(t1_s, 1)
                            dve.wait_ge(t1_s, g + 1)
                            dve.tensor_tensor(tg, psum[:, 4, :], tg, ALU.add).then_inc(t2_s, 1)
                            dve.wait_ge(n_s, g + 1)
                            if not first(it):
                                dve.wait_ge(stored[a], it * 16)
                            dve.tensor_tensor(tg, hT[:], ng, ALU.subtract).then_inc(d_s, 1)
                            dve.wait_ge(d_s, g + 1)
                            dve.tensor_tensor(tg, tg, zg, ALU.mult).then_inc(e_s, 1)
                            dve.wait_ge(e_s, g + 1)
                            dve.tensor_tensor(new[a], tg, ng, ALU.add).then_inc(new_s, 1)
                            dve.wait_ge(new_s, g + 1)
                            dve.bn_stats(bn_st[:, bass.ds(g, 1), :].rearrange("p a c -> p (a c)"),
                                         new[a]).then_inc(bn_s, 1)
                    body(0)
                    with dve.Fori(1, GROUPS // 2) as it:
                        body(it)

                    dve.wait_ge(bn_s, GROUPS)
                    dve.bn_stats(bn_st[:, GROUPS - 1, :], new[(GROUPS - 1) % 2][:, 0:TAIL]).then_inc(bn_s, 1)
                    dve.wait_ge(bn_s, GROUPS + 1)

                @block.tensor
                def _(pe):
                    pe.wait_ge(w_ld, 64)
                    with pe.Fori(0, GROUPS // 2) as it:
                        for a in range(2):
                            g = it * 2 + a
                            for k in range(J):
                                if k == 0:
                                    pe.wait_ge(loaded[a], it * 32 + 32)
                                pe.transpose(psum[:, 1, k * P:(k + 1) * P], gd[:, a, k, :], ident[:])
                            for k in range(J):
                                pe.wait_ge(h_s, g * J + (k + 1))
                                mm = pe.transpose(psum[:, 0, k * P:(k + 1) * P], hs[:, a, k, :], ident[:])
                            mm.then_inc(tr_s, 1)
                            pe.wait_ge(ev_s, g * 2 + 2)
                            for q, (bank, src_m) in enumerate(((2, "ih"), (3, "ih"), (4, "i"), (5, "h"))):
                                col = min(q, 2) * D
                                if "i" in src_m:
                                    mm = pe.matmul(psum[:, bank, :], wi[:, col:col + D], aT[:], start=True,
                                                   stop=src_m == "i")
                                if "h" in src_m:
                                    mm = pe.matmul(psum[:, bank, :], wh[:, col:col + D], hT[:],
                                                   start=src_m == "h", stop=True)
                            mm.then_inc(mm_s, 1)
            end_phase()


            last_phase("g4", x3)


        def every_engine_enters():
            with nc.Block() as block:
                for enter in (block.sync, block.gpsimd, block.scalar, block.vector, block.tensor):
                    enter(lambda eng: eng.sem_inc(passed, 1))

        with nc.If(nc.values_load(bad_i[0:1, 0:1], min_val=0, max_val=BAD_MAX) == 0), ExitStack() as own:
            every_engine_enters()
            sorted_program(own)
        with nc.If(nc.values_load(bad_i[0:1, 0:1], min_val=0, max_val=BAD_MAX) != 0), ExitStack() as own:
            every_engine_enters()
            general(own)

def kernel(**inputs):
    import numpy as _np
    import concourse.bacc as _bacc
    from concourse import mybir as _mybir
    from concourse.bass_utils import run_bass_kernel_spmd as _run

    def by_tile(a, fill):
        a = _np.asarray(a)
        pad = _np.full((EDGES - len(a),) + a.shape[1:], fill, a.dtype)
        a = _np.concatenate([a, pad]).reshape((TILES, P) + a.shape[1:])
        return _np.ascontiguousarray(_np.moveaxis(a, 0, 1)).reshape(P, -1)

    i = {k: _np.asarray(v) for k, v in inputs.items()}
    cols = lambda a, n: _np.ascontiguousarray(a.reshape(n, -1).T)
    arrays = {
        "x": _np.concatenate([i["x"], _np.zeros((ROWS - N_NODES, D), i["x"].dtype)]),
        "dst_next": by_tile(i["dst"][1:], PAD_DST),
        "type8_flat": _np.concatenate([i["edge_type_8"], _np.zeros(EDGES - N_EDGES, i["edge_type_8"].dtype)])[None],
        "src": by_tile(i["src"], 0), "dst": by_tile(i["dst"], PAD_DST),
        "dst_flat": _np.concatenate([i["dst"], _np.full(EDGES - N_EDGES, PAD_DST, i["dst"].dtype)])[None],
        "attr": by_tile(i["edge_attr_9"], 0), "type16": by_tile(i["edge_type_16"], 0),
        "type8": by_tile(i["edge_type_8"], 0).view(_np.int32),
        "w_rel": i["L0_gnn_weight"], "root": i["L0_gnn_root"], "bias": i["L0_gnn_bias"][None],
        "self_w": i["L1_gnn_self_weight"], "bases": i["L1_gnn_bases"],
        "base_w": i["L1_gnn_base_weights"].reshape(1, -1),
        **{f"w{k}": i[f"L2_gnn_w{k}"] for k in range(5)},
        "w_msg": i["L3_gnn_W_msg"], "b_msg": i["L3_gnn_b_msg"][None], "w_att": i["L3_gnn_W_att"].reshape(1, -1),
        "b_att": i["L3_gnn_b_att"][None], "w_ihT": _np.ascontiguousarray(i["L3_gnn_W_ih"].T),
        "b_ih": cols(i["L3_gnn_b_ih"], 3), "w_hhT": _np.ascontiguousarray(i["L3_gnn_W_hh"].T),
        "b_hh": cols(i["L3_gnn_b_hh"], 3), "gamma": i["L3_gnn_gamma"][:, None], "beta": i["L3_gnn_beta"][:, None],
        "sph": spherical_constants(), "sph_cols": spherical_columns(),
    }
    nc = _bacc.Bacc("TRN2", target_bir_lowering=False, num_devices=1)
    feed, args = {}, {}
    for name, a in arrays.items():
        a = _np.ascontiguousarray(a)
        dt = I32 if a.dtype == _np.int32 else F32
        feed[f"in_{name}"] = a
        args[name] = nc.dram_tensor(f"in_{name}", a.shape, dt, kind="ExternalInput").ap()
    out = nc.dram_tensor("out_x", (ROWS, D), F32, kind="ExternalOutput").ap()
    build(nc, out=out, **args)
    r = _run(nc, [feed], core_ids=[0])
    return r.results[0]["out_x"][:N_NODES]
```
